# Optimizing a Trainium2 kernel written in Bass

```python
import numpy as np
import jax
import jax.numpy as jnp

def _softmax(x, axis=-1):
    return jax.nn.softmax(x, axis=axis)

def _gelu(x):
    return jax.nn.gelu(x, approximate=True)

def _silu(x):
    return jax.nn.silu(x)

def _sigmoid(x):
    return jax.nn.sigmoid(x)

def _layernorm(x, axis=-1, eps=1e-05):
    m = jnp.mean(x, axis=axis, keepdims=True)
    v = jnp.var(x, axis=axis, keepdims=True)
    return (x - m) / jnp.sqrt(v + eps)

def _scatter_add(tgt, idx, src, axis=0):
    return tgt.at[idx].add(src)

def _segment_sum(src, seg, n):
    return jax.ops.segment_sum(src, seg, n)
kernel_name = 'mk_gnn_resnorm_d2_gnn_r8_aa1f7c'

def setup_inputs(seed: int=0):
    np.random.seed(seed)
    _w = jnp.asarray

    def _rec_inputs():
        import jax
        import jax.numpy as jnp
        _gk = jax.random.key(seed)
        x = -0.0006008 + 1.001 * jax.random.normal(jax.random.fold_in(_gk, 1), (6250, 128), jnp.float32)
        _s = jax.random.randint(jax.random.fold_in(_gk, 2), (50000,), 0, 6250, jnp.int32)
        _d = jax.random.randint(jax.random.fold_in(_gk, 3), (50000,), 0, 6250, jnp.int32)
        _loop = jnp.arange(6250, dtype=jnp.int32)
        src = jnp.concatenate([_s, _d, _loop])
        dst = jnp.concatenate([_d, _s, _loop])
        _o = jnp.argsort(dst, stable=True)
        src = src[_o]
        dst = dst[_o]
        edge_attr_20 = jax.random.uniform(jax.random.fold_in(_gk, 12), (106250, 20), jnp.float32, 0.0, 1)
        edge_weight = jax.random.uniform(jax.random.fold_in(_gk, 14), (106250,), jnp.float32, 0.0, 0.999998)
        return (x, src, dst, edge_attr_20, edge_weight)
    x, src, dst, edge_attr_20, edge_weight = _rec_inputs()

    def _L0_gnn_setup():
        import jax, jax.numpy as jnp
        import numpy as np
        N_ATOMS = 2500
        N_PAIRS = 80000
        N_BASIS = 128
        N_FILTERS = 128
        N_RBF = 20

        def ssp(v):
            return jax.nn.softplus(v) - jnp.log(2.0)
        key = jax.random.key(seed)
        ks = jax.random.split(key, 16)
        s = 0.05
        return {'x': jax.random.normal(ks[0], (N_ATOMS, N_BASIS), dtype=jnp.float32), 'f_ij': jax.random.uniform(ks[1], (N_PAIRS, N_RBF), dtype=jnp.float32), 'rcut_ij': jax.random.uniform(ks[2], (N_PAIRS,), dtype=jnp.float32), 'idx_i': jax.random.randint(ks[3], (N_PAIRS,), 0, N_ATOMS), 'idx_j': jax.random.randint(ks[4], (N_PAIRS,), 0, N_ATOMS), 'W_in': jax.random.normal(ks[5], (N_BASIS, N_FILTERS), dtype=jnp.float32) * s, 'b_in': jnp.zeros((N_FILTERS,), dtype=jnp.float32), 'Wf1': jax.random.normal(ks[6], (N_RBF, N_FILTERS), dtype=jnp.float32) * s, 'bf1': jnp.zeros((N_FILTERS,), dtype=jnp.float32), 'Wf2': jax.random.normal(ks[7], (N_FILTERS, N_FILTERS), dtype=jnp.float32) * s, 'bf2': jnp.zeros((N_FILTERS,), dtype=jnp.float32), 'Wo1': jax.random.normal(ks[8], (N_FILTERS, N_BASIS), dtype=jnp.float32) * s, 'bo1': jnp.zeros((N_BASIS,), dtype=jnp.float32), 'Wo2': jax.random.normal(ks[9], (N_BASIS, N_BASIS), dtype=jnp.float32) * s, 'bo2': jnp.zeros((N_BASIS,), dtype=jnp.float32)}
    _L0_gnn_all = _L0_gnn_setup()
    _L0_gnn_in = {k: v for k, v in _L0_gnn_all.items() if k in ('W_in', 'b_in', 'Wf1', 'bf1', 'Wf2', 'bf2', 'Wo1', 'bo1', 'Wo2', 'bo2')}
    del _L0_gnn_all

    def _L1_gnn_setup():
        import jax, jax.numpy as jnp
        import numpy as np
        N_NODES = 12500
        N_EDGES = 400000
        D_IN = 128
        D_HID = 128

        def _sage_conv(x, src, dst, Wl, bl, Wr, n_nodes):
            agg = jax.ops.segment_sum(x[src], dst, num_segments=n_nodes)
            cnt = jax.ops.segment_sum(jnp.ones((src.shape[0],), x.dtype), dst, num_segments=n_nodes)
            mean = agg / jnp.maximum(cnt, 1.0)[:, None]
            return mean @ Wl.T + bl + x @ Wr.T
        key = jax.random.key(seed)
        ks = jax.random.split(key, 9)
        x = jax.random.normal(ks[0], (N_NODES, D_IN), dtype=jnp.float32)
        edge_index = jax.random.randint(ks[1], (2, N_EDGES), 0, N_NODES, dtype=jnp.int64)
        s = 1.0 / np.sqrt(D_IN)
        Wl1 = jax.random.uniform(ks[2], (D_HID, D_IN), jnp.float32, -s, s)
        bl1 = jax.random.uniform(ks[3], (D_HID,), jnp.float32, -s, s)
        Wr1 = jax.random.uniform(ks[4], (D_HID, D_IN), jnp.float32, -s, s)
        s2 = 1.0 / np.sqrt(D_HID)
        Wl2 = jax.random.uniform(ks[5], (D_HID, D_HID), jnp.float32, -s2, s2)
        bl2 = jax.random.uniform(ks[6], (D_HID,), jnp.float32, -s2, s2)
        Wr2 = jax.random.uniform(ks[7], (D_HID, D_HID), jnp.float32, -s2, s2)
        return {'x': x, 'edge_index': edge_index, 'Wl1': Wl1, 'bl1': bl1, 'Wr1': Wr1, 'Wl2': Wl2, 'bl2': bl2, 'Wr2': Wr2}
    _L1_gnn_all = _L1_gnn_setup()
    _L1_gnn_in = {k: v for k, v in _L1_gnn_all.items() if k in ('Wl1', 'bl1', 'Wr1', 'Wl2', 'bl2', 'Wr2')}
    del _L1_gnn_all
    return {'x': x, 'src': src, 'dst': dst, 'edge_attr_20': edge_attr_20, 'edge_weight': edge_weight, 'L0_gnn_W_in': _L0_gnn_in['W_in'], 'L0_gnn_b_in': _L0_gnn_in['b_in'], 'L0_gnn_Wf1': _L0_gnn_in['Wf1'], 'L0_gnn_bf1': _L0_gnn_in['bf1'], 'L0_gnn_Wf2': _L0_gnn_in['Wf2'], 'L0_gnn_bf2': _L0_gnn_in['bf2'], 'L0_gnn_Wo1': _L0_gnn_in['Wo1'], 'L0_gnn_bo1': _L0_gnn_in['bo1'], 'L0_gnn_Wo2': _L0_gnn_in['Wo2'], 'L0_gnn_bo2': _L0_gnn_in['bo2'], 'L1_gnn_Wl1': _L1_gnn_in['Wl1'], 'L1_gnn_bl1': _L1_gnn_in['bl1'], 'L1_gnn_Wr1': _L1_gnn_in['Wr1'], 'L1_gnn_Wl2': _L1_gnn_in['Wl2'], 'L1_gnn_bl2': _L1_gnn_in['bl2'], 'L1_gnn_Wr2': _L1_gnn_in['Wr2']}

def reference(x, src, dst, edge_attr_20, edge_weight, L0_gnn_W_in, L0_gnn_b_in, L0_gnn_Wf1, L0_gnn_bf1, L0_gnn_Wf2, L0_gnn_bf2, L0_gnn_Wo1, L0_gnn_bo1, L0_gnn_Wo2, L0_gnn_bo2, L1_gnn_Wl1, L1_gnn_bl1, L1_gnn_Wr1, L1_gnn_Wl2, L1_gnn_bl2, L1_gnn_Wr2):
    import jax
    import jax.numpy as jnp

    def _L0_gnn_ref(x, f_ij, rcut_ij, idx_i, idx_j, W_in, b_in, Wf1, bf1, Wf2, bf2, Wo1, bo1, Wo2, bo2):
        import jax, jax.numpy as jnp
        import numpy as np
        N_ATOMS = 2500
        N_PAIRS = 80000
        N_BASIS = 128
        N_FILTERS = 128
        N_RBF = 20

        def ssp(v):
            return jax.nn.softplus(v) - jnp.log(2.0)
        n_atoms = x.shape[0]
        h = x @ W_in + b_in
        Wij = ssp(f_ij @ Wf1 + bf1) @ Wf2 + bf2
        Wij = Wij * rcut_ij[:, None]
        x_ij = h[idx_j] * Wij
        agg = jax.ops.segment_sum(x_ij, idx_i, num_segments=n_atoms)
        out = ssp(agg @ Wo1 + bo1) @ Wo2 + bo2
        return out

    def _L1_gnn_ref(x, edge_index, Wl1, bl1, Wr1, Wl2, bl2, Wr2):
        import jax, jax.numpy as jnp
        import numpy as np
        N_NODES = 12500
        N_EDGES = 400000
        D_IN = 128
        D_HID = 128

        def _sage_conv(x, src, dst, Wl, bl, Wr, n_nodes):
            agg = jax.ops.segment_sum(x[src], dst, num_segments=n_nodes)
            cnt = jax.ops.segment_sum(jnp.ones((src.shape[0],), x.dtype), dst, num_segments=n_nodes)
            mean = agg / jnp.maximum(cnt, 1.0)[:, None]
            return mean @ Wl.T + bl + x @ Wr.T
        src, dst = (edge_index[0], edge_index[1])
        n = x.shape[0]
        h = jax.nn.relu(_sage_conv(x, src, dst, Wl1, bl1, Wr1, n))
        h = jax.nn.relu(_sage_conv(h, src, dst, Wl2, bl2, Wr2, n))
        return h
    edge_index = jnp.stack([src, dst])
    x = _layernorm(x + _L0_gnn_ref(x, edge_attr_20, edge_weight, src, dst, L0_gnn_W_in, L0_gnn_b_in, L0_gnn_Wf1, L0_gnn_bf1, L0_gnn_Wf2, L0_gnn_bf2, L0_gnn_Wo1, L0_gnn_bo1, L0_gnn_Wo2, L0_gnn_bo2), axis=-1)
    x = _layernorm(x + _L1_gnn_ref(x, edge_index, L1_gnn_Wl1, L1_gnn_bl1, L1_gnn_Wr1, L1_gnn_Wl2, L1_gnn_bl2, L1_gnn_Wr2), axis=-1)
    return x

_drawn_inputs = setup_inputs


def setup_inputs(seed=0):
    import zlib

    import numpy as np

    out = dict(_drawn_inputs(seed))
    spreads = {'L0_gnn_b_in': (0.0, 0.526),
     'L0_gnn_bf1': (0.0, 0.8),
     'L0_gnn_bf2': (0.0, 1.104),
     'L0_gnn_bo1': (0.0, 2.0),
     'L0_gnn_bo2': (0.0, 2.0)}
    factors = {'edge_attr_20': 8.0,
     'edge_weight': 4.435,
     'L0_gnn_Wf1': 6.487,
     'L0_gnn_Wf2': 6.019,
     'L1_gnn_bl1': 3.267}
    for name, (base, spread) in spreads.items():
        noise = np.random.default_rng([zlib.crc32(name.encode()), seed]).standard_normal(out[name].shape)
        drawn = base * np.exp(spread * noise) if base else spread * noise
        out[name] = jnp.asarray(drawn.astype(out[name].dtype))
    for name, factor in factors.items():
        out[name] = (out[name] * factor).astype(out[name].dtype)
    return out
```

```python
from contextlib import ExitStack

import numpy as np

import concourse.bass as bass
from concourse import mybir

F32 = mybir.dt.float32
BF16 = mybir.dt.bfloat16
I32 = mybir.dt.int32
ALU = mybir.AluOpType
ACT = mybir.ActivationFunctionType

P = 128
LOG2 = float(np.log(2.0))
CAP = 20.0
EPS = 1e-5
NO_NODE = float(1 << 20)


def gnn_program(nc, x, src, dst, edge_attr, edge_weight, W_in, b_in, Wf1, bf1, Wf2, bf2, Wo1, bo1,
                Wo2, bo2, Wl1, bl1, Wr1, Wl2, bl2, Wr2, out):
    N, F = x.shape
    E, K = edge_attr.shape
    assert F == P
    T = -(-E // P)
    U = 8
    Q = -(-T // (4 * U)) * U
    NI = Q // U
    TP = 4 * Q
    NW = -(-N // P)
    GW = 7
    NG = NW // GW
    assert NW == NG * GW and N % P
    NP = NW * P
    AW = NP + P
    SL = -(-T // P)
    assert SL == GW and SL * P >= TP
    FULLT = E // P
    REST = E - FULLT * P
    FULLQ = E // (4 * P)
    RESTQ = E - FULLQ * 4 * P
    assert 0 < REST and FULLQ == Q - 1

    C = 4
    def internal(name, shape):
        return nc.dram_tensor(name, shape, F32, kind="Internal").ap()

    h_dram = internal("h_dram", [NP, F])
    x1_dram = internal("x1_dram", [NP, F])
    h1_dram = internal("h1_dram", [NP, F])
    rows_dram = internal("rows_dram", [NP, F])
    acc_dram = [internal(f"acc_dram{j}", [AW, F]) for j in range(C)]

    with ExitStack() as ctx:
        def sb(name, shape, dt=F32):
            return ctx.enter_context(nc.sbuf_tensor(name, shape, dt))

        def sem(name):
            return ctx.enter_context(nc.semaphore(name))

        x_sb = sb("x_sb", [P, NW, F])
        root = sb("root", [P, AW])
        aggT = sb("aggT", [P, AW])
        idx = sb("idx", [P, SL * P], I32)
        idx_dst = sb("idx_dst", [P, SL * P], I32)
        layer0 = sb("layer0", [P, 3, SL * P])
        weight = layer0[:, 0, :]
        src_col = layer0[:, 1, :]
        spare = layer0[:, 2, :]
        slot = sb("slot", [P, SL * P])
        meta = sb("meta", [P, 2, SL * P])
        first_row = sb("first_row", [1, SL * P], I32)
        rowsD = sb("rowsD", [P, NW + 1, F])
        ident = sb("ident", [P, P])
        iota_row = sb("iota_row", [P, P])
        iota_col = sb("iota_col", [P, 1])
        tri_incl0 = sb("tri_incl0", [P, P])
        tri_strict = sb("tri_strict", [P, P])
        shift = sb("shift", [P, P])
        corner = sb("corner", [P, P])
        ones = sb("ones", [P, P])
        wraw = sb("wraw", [P, 4, F])
        wT = sb("wT", [P, 4, F])
        w_in = sb("w_in", [P, F])
        wf1 = sb("wf1", [K + 1, F])
        wf2 = sb("wf2", [P, F])
        wo1 = sb("wo1", [P, F])
        wo2 = sb("wo2", [P, F])
        bo1c = sb("bo1c", [P, 1])
        cap_bo1 = sb("cap_bo1", [P, 1])
        bo1_log2 = sb("bo1_log2", [P, 1])
        cap_col = sb("cap_col", [P, 1])
        half_col = sb("half_col", [P, 1])
        eps_col = sb("eps_col", [P, 1])
        NB = 5
        bias3 = sb("bias3", [3, NB, F])
        bres = sb("bres", [3, 2, NB, F])
        bpart = sb("bpart", [3, 3, NB, F], BF16)
        brow = sb("brow", [3, NB, 4, F], BF16)
        tri_le = sb("tri_le", [P, P])
        ones3 = sb("ones3", [3, P], BF16)
        f_sb = sb("f_sb", [P, U, 4 * K])
        fT = sb("fT", [K + 1, 2, 4 * P])
        act_buf = sb("act_buf", [P, 4, 4 * P])
        soft, act_s = act_buf[:, 0:2, :], act_buf[:, 2:4, :]
        hg = sb("hg", [P, U, 4, F])
        hot = sb("hot", [P, 2, 4, P])
        src_row = sb("src_row", [P, 2, 4 * P], I32)
        rank = sb("rank", [P, 2, 4])
        other = sb("other", [P, 2, 4])
        add_idx = sb("add_idx", [P, 2, 4], I32)
        idx_stage = sb("idx_stage", [P, 2, 16], I32)
        sums = sb("sums", [P, 2, 4, F])
        meta_stage = sb("meta_stage", [P, 2, 4, 2])
        ring = hg[:, :, :, :].rearrange("p u j f -> p (u j f)")
        copies = ring[:, 0:C * GW * F].rearrange("p (k w f) -> p k w f", k=C, f=F)
        rowsN = ring[:, 0:2 * GW * F].rearrange("p (b w f) -> p b w f", b=2, f=F)
        nS = act_buf[:, :, :].rearrange("p b c -> p (b c)")[:, 0:2 * GW * F].rearrange("p (b c) -> p b c", b=2)
        agg_n = aggT[:, 0:2 * GW * F].rearrange("p (b w f) -> p b w f", b=2, f=F)
        xT = ring[:, 0:GW * F]
        nT = aggT[:, 2 * GW * F:3 * GW * F]
        gT = sums[:, :, :, :].rearrange("p b j f -> p (b j f)")[:, 0:GW * F]
        yv = layer0[:, 1:3, :].rearrange("p b (w f) -> p b w f", f=F)
        yT = layer0[:, 0, :].rearrange("p (w f) -> p w f", f=F)
        stats = sb("stats", [P, GW, 6])
        mv = sb("mv", [P, GW, 2])
        rs = sb("rs", [P, 4, GW])
        metaD = sb("metaD", [P, NW, 2])
        endD = sb("endD", [P, NW + 1])
        cntD = sb("cntD", [P, 3, NW])
        node_id = sb("node_id", [P, NW], I32)
        small = sb("small", [P, 4, SL])
        prev_i = sb("prev_i", [P, SL], I32)
        prev_f = sb("prev_f", [P, SL])

        ps = ctx.enter_context(nc.psum_tensor("ps", [P, 8, 512], F32))

        def wide(k):
            return ps[:, 2 * k:2 * k + 2, :].rearrange("p b c -> p (b c)")

        dst_i = root[:, 0:896].bitcast(I32)
        src_i = root[:, 896:1792].bitcast(I32)
        ew_te = root[:, 1792:2688]
        dst_te = root[:, 2688:3584]
        start_te = root[:, 3584:4480]
        id_te = root[:, 4480:5376]
        end_te = root[:, 5376:6272]
        rowsD_flat = rowsD[:, :, :].rearrange("p w f -> p (w f)")
        last_te, src_te, valid, edge_no = (rowsD_flat[:, k * SL * P:(k + 1) * SL * P] for k in range(4))
        meta_row = rowsD_flat[0:2, :]

        def te(v):
            return v.rearrange("p (s e) -> p s e", e=P)

        s = {}
        names = """loads consts w_loads pads x_pad chainv chaina chainp te_ready te_psum te_copied
            tot_ready pref_ready first_ready first_psum slot_psum wt_psum wt_ready
            bias_ready xt_psum xt_sb h_psum h_sb h_stored zero_agg zero_rows zero_meta
            ft_ready ft_copied z1_ready soft_done ssp_done z2_ready x_ready hot_ready 
            f_rest src_rest meta_staged meta_copied
            md_psum md_sb cnt_psum ids_ready sums_ready sums_copied sums_sb
            adds_begun add_idx_ready other_ready src_loaded0 src_loaded1""".split()
        for n in names:
            s[n] = sem(n)
        f_loaded = [sem(f"f_loaded{u}") for u in range(U)]
        gathered = [sem(f"gathered{u}") for u in range(U)]
        added = [sem(f"added{j}") for j in range(C)]
        idx_staged = [sem(f"idx_staged{l}") for l in range(3)]
        hot_rdy = [s["hot_ready"], sem("hot_ready1"), sem("hot_ready2")]
        agg_rdy = [s["sums_ready"], sem("agg_ready1"), sem("agg_ready2")]
        acc_dn = [None, sem("acc_done1"), sem("acc_done2")]
        agg_clear = [s["zero_agg"], sem("agg_clear1"), sem("agg_clear2")]
        scattered = [sem(f"scattered{g}") for g in range(NG)]
        of_layers = {"stored0 stored1 y_done": (0, 1, 2),
                     "rows_psum rows_sb": (1, 2), "rows_loaded0 rows_loaded1": (0, 1, 2),
                     "rows_summed agg_psum agg_sb nt_psum nt_soft ssp out_psum sum_done": (0,),
                     "var_done rstd": (0, 2),
                     "relu_in": (1, 2),
                     "yt_psum yt_sb root_psum root_done": (0, 1)}
        node = [{n: sem(f"{n}_{l}") for ns, ls in of_layers.items() if l in ls for n in ns.split()} for l in range(3)]

        block = ctx.enter_context(nc.Block())

        def edge_steps(eng, skew, step):
            for u in range(U):
                step(0, u)
            with eng.Fori(1, NI) as i:
                for u in range(U):
                    step(i, u)
            for u in range(skew):
                step(NI, u)

        def back(i, u, k):
            d = u - k
            i, u = i + d // U, d % U
            if isinstance(i, int) and not 0 <= i < NI:
                return None
            return i, u, i * U + u

        def load_firsts(eng, regs, q):
            eng.load(regs, first_row[0:1, bass.ds(4 * q, 4)])
            return [eng.snap(r, min_val=0, max_val=N) for r in regs]

        def later(q, n):
            return not isinstance(q, int) or q >= n

        @block.sync
        def _(sp):
            whole = (SL - 1) * P
            part = FULLT - whole
            sp.wait_ge(s["pads"], 1)
            for v, d in ((dst_i, dst), (src_i, src), (ew_te, edge_weight)):
                t3 = te(v)
                sp.dma_start(t3[:, 0:SL - 1, :], d[0:whole * P].rearrange("(s t e) -> t s e", t=P, e=P)).then_inc(s["loads"], 16)
                sp.dma_start(t3[0:part, SL - 1, :], d[whole * P:FULLT * P].rearrange("(t e) -> t e", e=P)).then_inc(s["loads"], 16)
                sp.dma_start(t3[part:part + 1, SL - 1, 0:REST], d[FULLT * P:E].rearrange("(t e) -> t e", t=1)).then_inc(s["loads"], 16)
            d2 = dst[0:FULLT * P].rearrange("(t e) -> t e", e=P)[:, P - 1:P]
            sp.dma_start(prev_i[1:P, 0:1], d2[0:P - 1, :], allow_slow_non_contiguous=True).then_inc(s["loads"], 16)
            for sl in range(1, SL):
                n = min(P, FULLT - (sl * P - 1))
                sp.dma_start(prev_i[0:n, sl:sl + 1], d2[sl * P - 1:sl * P - 1 + n, :],
                             allow_slow_non_contiguous=True).then_inc(s["loads"], 16)
            sp.wait_ge(s["x_pad"], 1)
            sp.dma_start(x_sb[:, 0:NW - 1, :], x[0:(NW - 1) * P, :].rearrange("(w p) f -> p w f", p=P)).then_inc(s["w_loads"], 16)
            sp.dma_start(x_sb[0:N - (NW - 1) * P, NW - 1, :], x[(NW - 1) * P:N, :]).then_inc(s["w_loads"], 16)
            for t, d in ((w_in, W_in), (wf2, Wf2), (wo1, Wo1), (wo2, Wo2), (wraw[:, 0, :], Wl1),
                         (wraw[:, 1, :], Wr1), (wraw[:, 2, :], Wl2), (wraw[:, 3, :], Wr2), (wf1[0:K, :], Wf1)):
                sp.dma_start(t[:, :], d).then_inc(s["w_loads"], 16)
            sp.dma_start(wf1[K:K + 1, :], bf1.rearrange("(a f) -> a f", a=1)).then_inc(s["w_loads"], 16)
            sp.dma_start(bo1c[:, :], bo1.rearrange("(f a) -> f a", a=1), allow_slow_non_contiguous=True).then_inc(s["w_loads"], 16)
            for n, b in enumerate((b_in, bf2, bo2, bl1, bl2)):
                for r in range(3):
                    sp.dma_start(bias3[r:r + 1, n, :], b.rearrange("(a f) -> a f", a=1)).then_inc(s["w_loads"], 16)
            sp.wait_ge(s["zero_agg"], 1)
            sp.dma_start(rows_dram.rearrange("(p w) f -> p (w f)", p=P), aggT[:, 0:NP]).then_inc(s["zero_rows"], 16)
            for a in acc_dram:
                sp.dma_start(a.rearrange("(p w) f -> p (w f)", p=P), aggT[:, :]).then_inc(s["zero_rows"], 16)
            for g in range(NG):
                sp.wait_ge(s["h_sb"], g + 1)
                sp.dma_start(h_dram[g * GW * P:(g + 1) * GW * P, :].rearrange("(w p) f -> p w f", p=P),
                             rowsD[:, g * GW:(g + 1) * GW, :]).then_inc(s["h_stored"], 16)

            f_v = edge_attr[0:FULLQ * 4 * P, :].rearrange("(q p a) k -> q p (a k)", p=P, a=4)

            def load_features(i, u):
                q = i * U + u
                if later(q, U):
                    sp.wait_ge(s["ft_ready"], q - U + 1)
                if isinstance(q, int) and q == FULLQ:
                    fp = RESTQ // 4
                    e0 = FULLQ * 4 * P
                    sp.dma_start(f_sb[fp:fp + 1, u, 0:(RESTQ % 4) * K],
                                 edge_attr[e0 + 4 * fp:E, :].rearrange("(p a) k -> p (a k)", p=1)).then_inc(s["f_rest"], 16)
                    sp.wait_ge(s["f_rest"], 16)
                    sp.dma_start(f_sb[0:fp, u, :], edge_attr[e0:e0 + 4 * fp, :].rearrange("(p a) k -> p (a k)", a=4)).then_inc(f_loaded[u], 16)
                elif isinstance(q, int):
                    sp.dma_start(f_sb[:, u, :], f_v[q]).then_inc(f_loaded[u], 16)
                else:
                    sp.dma_start(f_sb[:, u, :], f_v[bass.ds(q, 1)].rearrange("a p k -> (a p) k")).then_inc(f_loaded[u], 16)

            def load_sources(i, u):
                q = i * U + u
                if later(q, 2):
                    sp.wait_ge(s["hot_ready"], q - 1)
                n = RESTQ if isinstance(q, int) and q == FULLQ else 4 * P
                row = src[bass.ds(q * 4 * P, n)].rearrange("(a e) -> a e", a=1)
                sp.dma_start(src_row[:, u % 2, 0:n], row.broadcast_to([P, n])).then_inc(s[f"src_loaded{u % 2}"], 16)

            for u in range(4):
                load_features(0, u)
            for u in range(4):
                load_features(0, u + 4)
                load_sources(0, u)
            with sp.Fori(1, NI - 1) as i:
                for u in range(4):
                    load_features(i, u)
                    load_sources(i - 1, u + 4)
                for u in range(4):
                    load_features(i, u + 4)
                    load_sources(i, u)
            for u in range(4):
                load_features(NI - 1, u)
                load_sources(NI - 2, u + 4)
            for u in range(4):
                load_features(NI - 1, u + 4)
                load_sources(NI - 1, u)
            for u in range(4):
                load_sources(NI - 1, u + 4)

            def node_traffic(l, target):
                n = node[l]
                for g in range(NG + 1):
                    if g < NG:
                        if l == 0:
                            if g >= 1:
                                sp.wait_ge(n["rows_summed"], 3 * g)
                            for k in range(C):
                                sp.dma_start(copies[:, k], acc_dram[k][g * GW * P:(g + 1) * GW * P, :]
                                             .rearrange("(w p) f -> p w f", p=P)).then_inc(n[f"rows_loaded{g % 2}"], 16)
                    if g < NG and l > 0:
                        sp.wait_ge(scattered[g], 16 * GW * l)
                        if g >= 2:
                            sp.wait_ge(n["relu_in"], g - 1)
                        sp.dma_start(rowsN[:, g % 2], rows_dram[g * GW * P:(g + 1) * GW * P, :]
                                     .rearrange("(w p) f -> p w f", p=P)).then_inc(n[f"rows_loaded{g % 2}"], 16)
                    h = g - 1
                    if h >= 0:
                        sp.wait_ge(n["y_done"], h + 1)
                        if target is out:
                            sp_store_out(h, n)
                        else:
                            sp.dma_start(target[h * GW * P:(h + 1) * GW * P, :].rearrange("(w p) f -> p w f", p=P),
                                         x_sb[:, h * GW:(h + 1) * GW, :] if l == 0 else yv[:, h % 2]).then_inc(n[f"stored{h % 2}"], 16)

            def sp_store_out(h, n):
                w0 = h * GW
                full = min(GW, NW - 1 - w0)
                sp.dma_start(out[w0 * P:(w0 + full) * P, :].rearrange("(w p) f -> p w f", p=P),
                             yv[:, h % 2, 0:full, :]).then_inc(n[f"stored{h % 2}"], 16)
                if full < GW:
                    sp.dma_start(out[(NW - 1) * P:N, :], yv[0:N - (NW - 1) * P, h % 2, full, :]).then_inc(n[f"stored{h % 2}"], 16)

            for j in range(C):
                sp.wait_ge(added[j], 16 * Q)
            node_traffic(0, x1_dram)
            node_traffic(1, h1_dram)
            node_traffic(2, out)
            sp.wait_ge(node[2]["stored0"], 16 * (NG - NG // 2 + 1))
            sp.wait_ge(node[2]["stored1"], 16 * (NG // 2))

        quads_begun = sem("quads_begun")

        @block.gpsimd
        def _(pool):
            def const(ins):
                ins.then_inc(s["chainp"], 1)
                const.n += 1
                pool.wait_ge(s["chainp"], const.n)
            const.n = 0
            const(nc.gpsimd.memset(prev_i[:, :], 0))
            nc.gpsimd.memset(root[:, 0:2688].bitcast(I32), 0).then_inc(s["pads"], 1)
            const(nc.gpsimd.memset(ident[:, :], 0.0))
            const(nc.gpsimd.affine_select(out=ident[:, :], in_=ident[:, :], compare_op=ALU.not_equal, fill=1.0,
                                          base=0, pattern=[[-1, P]], channel_multiplier=1))
            const(nc.gpsimd.memset(ones[:, :], 1.0))
            const(nc.gpsimd.affine_select(out=tri_incl0[:, :], in_=ones[:, :], compare_op=ALU.is_ge, fill=0.0,
                                          base=0, pattern=[[1, P]], channel_multiplier=-1))
            const(nc.gpsimd.memset(tri_incl0[0:1, :], 0.0))
            const(nc.gpsimd.affine_select(out=tri_le[:, :], in_=ones[:, :], compare_op=ALU.is_ge, fill=0.0,
                                          base=0, pattern=[[-1, P]], channel_multiplier=1))
            const(nc.gpsimd.affine_select(out=tri_strict[:, :], in_=ones[:, :], compare_op=ALU.is_gt, fill=0.0,
                                          base=0, pattern=[[1, P]], channel_multiplier=-1))
            const(nc.gpsimd.affine_select(out=shift[:, :], in_=ones[:, :], compare_op=ALU.is_equal, fill=0.0,
                                          base=-1, pattern=[[1, P]], channel_multiplier=-1))
            const(nc.gpsimd.affine_select(out=corner[:, :], in_=ones[:, :], compare_op=ALU.is_equal, fill=0.0,
                                          base=P - 1, pattern=[[1, P]], channel_multiplier=-1))
            const(nc.gpsimd.iota(te(edge_no), pattern=[[P * P, SL], [1, P]], base=0, channel_multiplier=P,
                                 allow_small_or_imprecise_dtypes=True))
            const(nc.gpsimd.iota(iota_row[:, :], pattern=[[1, P]], base=0, channel_multiplier=0,
                                 allow_small_or_imprecise_dtypes=True))
            nc.gpsimd.iota(iota_col[:, :], pattern=[[0, 1]], base=0, channel_multiplier=1,
                           allow_small_or_imprecise_dtypes=True).then_inc(s["consts"], 1)

            LAG = 3

            def gather_and_add():
                pool.wait_ge(s["h_stored"], 16 * NG)
                pool.wait_ge(s["zero_rows"], 16 * (1 + C))

                def step(i, u):
                    c = back(i, u, 0)
                    if c:
                        q = c[2]
                        if u % 4 == 0:
                            pool.wait_ge(idx_staged[0], 2 * i + u // 4 + 1)
                        if later(q, U):
                            pool.wait_ge(s["sums_ready"], q - U + 1)
                        pool.sem_inc(quads_begun, 1)
                        for j in range(4):
                            nc.gpsimd.indirect_dma_start(
                                out=hg[:, u, j, :], out_offset=None, in_=h_dram[:, :],
                                in_offset=bass.IndirectOffsetOnAxis(ap=idx_stage[:, u // 4, 4 * (u % 4) + j:4 * (u % 4) + j + 1], axis=0),
                            ).then_inc(gathered[u], 16)
                    c = back(i, u, LAG)
                    if c:
                        _, v, q = c
                        pool.wait_ge(s["add_idx_ready"], q + 1)
                        pool.wait_ge(s["sums_sb"], q + 1)
                        for j in range(C):
                            if later(q, 1):
                                pool.wait_ge(added[j], 16 * q)
                            pool.sem_inc(s["adds_begun"], 1)
                            nc.gpsimd.indirect_dma_start(
                                out=acc_dram[j][:, :], out_offset=bass.IndirectOffsetOnAxis(ap=add_idx[:, v % 2, j:j + 1], axis=0),
                                in_=sums[:, v % 2, j, :], in_offset=None, compute_op=ALU.add,
                            ).then_inc(added[j], 16)
                edge_steps(pool, LAG, step)

            def gather(l, table, table_whole):
                for stored, count in table_whole:
                    pool.wait_ge(stored, count)

                def quad(i, u):
                    q = i * U + u
                    if u % 4 == 0:
                        pool.wait_ge(idx_staged[l], 2 * i + u // 4 + 1)
                    if later(q, U):
                        pool.wait_ge(agg_rdy[l], q - U + 1)
                    pool.sem_inc(quads_begun, 1)
                    for j in range(4):
                        nc.gpsimd.indirect_dma_start(
                            out=hg[:, u, j, :], out_offset=None, in_=table[:, :],
                            in_offset=bass.IndirectOffsetOnAxis(ap=idx_stage[:, u // 4, 4 * (u % 4) + j:4 * (u % 4) + j + 1], axis=0),
                        ).then_inc(gathered[u], 16)
                edge_steps(pool, 0, quad)

            def scatter(l):
                n = node[l]
                pool.wait_ge(s["ids_ready"], 1)
                pool.wait_ge(s["zero_rows"], 16)
                for g in range(NG):
                    pool.wait_ge(n["rows_sb"], g + 1)
                    for j in range(GW):
                        w = g * GW + j
                        nc.gpsimd.indirect_dma_start(
                            out=rows_dram[:, :], out_offset=bass.IndirectOffsetOnAxis(ap=node_id[:, w:w + 1], axis=0),
                            in_=rowsD[:, w, :], in_offset=None, bounds_check=NP - 1, oob_is_err=False,
                        ).then_inc(scattered[g], 16)

            gather_and_add()
            for k in range(NG):
                pool.wait_ge(node[0][f"rows_loaded{k % 2}"], 16 * C * (k // 2 + 1))
                if k >= 2:
                    pool.wait_ge(node[0]["agg_psum"], k - 1)
                for m, (a, b, o) in enumerate(((copies[:, 0], copies[:, 1], copies[:, 0]), (copies[:, 2], copies[:, 3], copies[:, 2]),
                                               (copies[:, 0], copies[:, 2], agg_n[:, k % 2]))):
                    nc.gpsimd.tensor_tensor(o, a, b, ALU.add).then_inc(node[0]["rows_summed"], 1)
                    if m:
                        pool.wait_ge(node[0]["rows_summed"], 3 * k + m + 1)
            gather(1, x1_dram, [(node[0]["stored0"], 16 * (NG - NG // 2)), (node[0]["stored1"], 16 * (NG // 2))])
            scatter(1)
            gather(2, h1_dram, [(node[1]["stored0"], 16 * (NG - NG // 2)), (node[1]["stored1"], 16 * (NG // 2))])
            scatter(2)

        @block.scalar
        def _(act):
            chain = [0]

            def link(ins):
                chain[0] += 1
                ins.then_inc(s["chaina"], 1)
                act.wait_ge(s["chaina"], chain[0])

            for n, t in enumerate((start_te, meta[:, 0, :], meta[:, 1, :], idx[:, :], weight[:, :], idx_dst[:, :])):
                act.wait_ge(s["te_psum"], n + 1)
                nc.scalar.copy(t, wide(n % 2)[:, 0:SL * P]).then_inc(s["te_copied"], 1)
            act.wait_ge(s["first_psum"], 1)
            nc.scalar.copy(first_row[:, :], wide(2)[0:1, 0:SL * P]).then_inc(s["first_ready"], 1)
            for g in range(NG):
                act.wait_ge(s["xt_psum"], g + 1)
                if g >= 1:
                    act.wait_ge(s["h_psum"], g)
                nc.scalar.copy(xT, wide(2)[:, 0:GW * P]).then_inc(s["xt_sb"], 1)

            def stage(l, i, half):
                if later(i, 1):
                    for u in range(4 * half, 4 * half + 4):
                        act.wait_ge(gathered[u], 64 * (NI * l + i))
                table = idx_dst if l == 0 else idx
                nc.scalar.copy(idx_stage[:, half, :], table[:, bass.ds(i * 32 + 16 * half, 16)]
                               ).then_inc(idx_staged[l], 1)

            act.wait_ge(s["te_copied"], 6)
            act.wait_ge(s["first_ready"], 1)
            stage(0, 0, 0)
            stage(0, 0, 1)

            def step(i, u):
                c = back(i, u, 4)
                if c:
                    _, v, q = c
                    act.wait_ge(s["sums_ready"], q + 1)
                    if later(q, 2):
                        for j in range(C):
                            act.wait_ge(added[j], 16 * (q - 1))
                    nc.scalar.copy(sums[:, v % 2], ps[:, 5 + v % 2, :].rearrange("p (j f) -> p j f", f=F)).then_inc(s["sums_sb"], 1)
                c = back(i, u, 0)
                if c:
                    _, _, q = c
                    act.wait_ge(s["ft_ready"], q + 1)
                    if later(q, 2):
                        act.wait_ge(s["z1_ready"], q - 1)
                    nc.scalar.copy(fT[0:K, u % 2, :].rearrange("k (p a) -> k a p", a=4),
                                   ps[0:K, 0, :].rearrange("k (a p) -> k a p", a=4)).then_inc(s["ft_copied"], 1)
                c = back(i, u, 1)
                if c:
                    _, v, q = c
                    z, t = ps[:, 1 + v % 2, :], soft[:, v % 2, :]
                    act.wait_ge(s["z1_ready"], q + 1)
                    if later(q, 2):
                        act.wait_ge(s["ssp_done"], q - 1)
                    nc.scalar.activation(t, z, ACT.Relu, bias=cap_col[:, :], scale=-1.0).then_inc(s["soft_done"], 1)
                    act.wait_ge(s["soft_done"], 3 * q + 1)
                    nc.scalar.activation(t, t, ACT.Exp, bias=cap_col[:, :], scale=-1.0).then_inc(s["soft_done"], 1)
                    act.wait_ge(s["soft_done"], 3 * q + 2)
                    nc.scalar.activation(t, t, ACT.Ln, bias=half_col[:, :], scale=0.5).then_inc(s["soft_done"], 1)
                if u == 4 and back(i, u, 0):
                    stage(0, i + 1, 0)
                if u == 0 and back(i, u, 0) and later(i, 1):
                    stage(0, i, 1)

            edge_steps(act, 4, step)

            def node_phase(l):
                n = node[l]
                if l < 2:
                    for u in range(U):
                        act.wait_ge(gathered[u], 64 * NI * (l + 1))
                    stage(l + 1, 0, 0)
                    stage(l + 1, 0, 1)
                if l == 1:
                    act.wait_ge(s["md_psum"], 1)
                    nc.scalar.copy(metaD[:, :, :].rearrange("p w c -> p (w c)"), ps[:, 7, 0:2 * NW]).then_inc(s["md_sb"], 1)
                    act.wait_ge(s["tot_ready"], 2)
                if l == 2:
                    for g in range(NG):
                        act.wait_ge(scattered[g], 16 * GW)
                for g in range(NG if l else 0):
                    act.wait_ge(n["rows_psum"], g + 1)
                    for j in range(GW):
                        w = g * GW + j
                        ins = nc.scalar.activation(rowsD[:, w, :], wide(g % 2)[:, j * F:(j + 1) * F],
                                                   ACT.Copy, scale=cntD[:, 2, w:w + 1])
                    ins.then_inc(n["rows_sb"], 1)
                for g in range(NG + 2):
                    if l == 0 and g < NG:
                        act.wait_ge(n["agg_psum"], g + 1)
                        if g >= 1:
                            act.wait_ge(n["nt_psum"], g)
                        nc.scalar.copy(gT[:, :], wide(1)[:, 0:GW * F]).then_inc(n["agg_sb"], 1)
                        act.wait_ge(n["nt_psum"], g + 1)
                        if g >= 1:
                            act.wait_ge(n["ssp"], g)
                        v = wide(2)[:, 0:GW * F]
                        link(nc.scalar.activation(nT[:, :], v, ACT.Relu, bias=cap_bo1[:, :], scale=-1.0))
                        link(nc.scalar.activation(nT[:, :], nT[:, :], ACT.Exp, bias=cap_col[:, :], scale=-1.0))
                        nc.scalar.activation(nT[:, :], nT[:, :], ACT.Ln, bias=half_col[:, :], scale=0.5).then_inc(n["nt_soft"], 1)
                    h = g - 1
                    if l != 1 and 0 <= h < NG:
                        act.wait_ge(n["var_done"], h + 1)
                        link(nc.scalar.activation(rs[:, 0, :], mv[:, :, 1], ACT.Ln, bias=eps_col[:, :]))
                        nc.scalar.activation(rs[:, 1, :], rs[:, 0, :], ACT.Exp, scale=-0.5).then_inc(n["rstd"], 1)
                    h = g - 2
                    if l < 2 and h >= 0:
                        act.wait_ge(n["yt_psum"], h + 1)
                        if h >= 1:
                            act.wait_ge(n["root_psum"], h)
                        nc.scalar.copy(yT[:, :, :].rearrange("p w f -> p (w f)"), wide(1)[:, 0:GW * F]).then_inc(n["yt_sb"], 1)
                        act.wait_ge(n["root_psum"], h + 1)
                        nc.scalar.copy(root[:, h * GW * F:(h + 1) * GW * F], wide(3)[:, 0:GW * F]).then_inc(n["root_done"], 1)
                if l < 2:
                    stage_edges(l + 1)

            act_regs = [act.alloc_register(f"act_first{j}") for j in range(4)]

            def stage_edges(l):
                def step(i, u):
                    c = back(i, u, 1)
                    if c and l == 1:
                        _, _, q = c
                        firsts = load_firsts(act, act_regs, q)
                        act.wait_ge(agg_rdy[1], q + 1)
                        for j in range(4):
                            if j or later(q, 1):
                                act.wait_ge(s["meta_copied"], 4 * q + j)
                            nc.scalar.copy(meta_row[:, bass.ds(firsts[j], P)], ps[0:2, 7, j * P:(j + 1) * P]
                                           ).then_inc(s["meta_copied"], 1)
                    c = back(i, u, 0)
                    if c and l == 1:
                        _, v, q = c
                        if later(q, 2):
                            act.wait_ge(agg_rdy[1], q - 1)
                        nc.scalar.copy(meta_stage[:, v % 2, :, :].rearrange("p j c -> p c j"),
                                       meta[:, :, bass.ds(4 * q, 4)]).then_inc(s["meta_staged"], 1)
                    if u == 4 and c:
                        stage(l, i + 1, 0)
                    if u == 0 and c and later(i, 1):
                        stage(l, i, 1)
                if l == 1:
                    act.wait_ge(s["zero_meta"], 1)
                edge_steps(act, 1, step)

            node_phase(0)
            node_phase(1)
            node_phase(2)

        @block.vector
        def _(dve):
            chain = [0]

            def link(ins):
                chain[0] += 1
                ins.then_inc(s["chainv"], 1)
                dve.wait_ge(s["chainv"], chain[0])

            def then_chain(ins):
                chain[0] += 1
                ins.then_inc(s["chainv"], 1)

            nc.vector.memset(x_sb[:, NW - 1, :], 0.0).then_inc(s["x_pad"], 1)
            nc.vector.memset(aggT[:, :], 0.0).then_inc(s["zero_agg"], 1)
            then_chain(nc.vector.memset(cap_col[:, :], CAP))
            then_chain(nc.vector.memset(half_col[:, :], 0.5))
            then_chain(nc.vector.memset(eps_col[:, :], EPS))
            then_chain(nc.vector.memset(ones3[:, :], 1.0))
            then_chain(nc.vector.memset(fT[:, :, :], 1.0))
            then_chain(nc.vector.memset(endD[:, :], 0.0))
            link(nc.vector.memset(prev_f[:, :], -1.0))
            dve.wait_ge(s["loads"], 16 * (9 + SL))
            dve.wait_ge(s["consts"], 1)
            e_no = edge_no
            then_chain(nc.vector.tensor_scalar(valid, e_no, float(E), None, ALU.is_lt))
            then_chain(nc.vector.tensor_copy(src_te, src_i))
            then_chain(nc.vector.tensor_copy(prev_f[:, :], prev_i[:, :]))
            link(nc.vector.tensor_copy(dst_te, dst_i))
            link(nc.vector.memset(prev_f[0:1, 0:1], -1.0))
            d3, c3, i3, l3 = te(dst_te), te(start_te), te(id_te), te(last_te)
            then_chain(nc.vector.tensor_tensor(c3[:, :, 1:P], d3[:, :, 1:P], d3[:, :, 0:P - 1], ALU.not_equal))
            then_chain(nc.vector.tensor_tensor(c3[:, :, 0], d3[:, :, 0], prev_f[:, :], ALU.not_equal))
            then_chain(nc.vector.tensor_tensor(l3[:, :, 0:P - 1], d3[:, :, 1:P], d3[:, :, 0:P - 1], ALU.not_equal))
            link(nc.vector.memset(l3[:, :, P - 1], 1.0))
            link(nc.vector.scalar_tensor_tensor(last_te, e_no, float(E - 1), last_te, ALU.is_equal, ALU.max))
            then_chain(nc.vector.tensor_tensor(i3[:, :, 1:P], c3[:, :, 1:P], d3[:, :, 1:P], ALU.mult))
            then_chain(nc.vector.tensor_copy(i3[:, :, 0], d3[:, :, 0]))
            link(nc.vector.scalar_tensor_tensor(end_te, e_no, 1.0, last_te, ALU.add, ALU.mult))
            link(nc.vector.tensor_tensor(start_te, start_te, valid, ALU.mult))
            link(nc.vector.tensor_reduce(small[:, 0, :], c3, mybir.AxisListType.X, ALU.add))
            link(nc.vector.memset(small[:, 1, 0:1], 0.0))
            for k in range(1, SL):
                link(nc.vector.tensor_tensor(small[:, 1, k:k + 1], small[:, 1, k - 1:k], small[:, 0, k - 1:k], ALU.add))
            nc.vector.tensor_tensor(small[:, 3, :], c3[:, :, 0], te(valid)[:, :, 0], ALU.subtract).then_inc(s["te_ready"], 1)
            dve.wait_ge(s["te_ready"], 1)
            dve.wait_ge(s["pref_ready"], 1)
            link(nc.vector.tensor_tensor(small[:, 2, :], ps[:, 6, 0:SL], small[:, 3, :], ALU.add))
            link(nc.vector.tensor_scalar(small[:, 2, :], small[:, 2, :], float(N), 0.0, ALU.min, ALU.max))
            nc.vector.tensor_copy(small[:, 0, :], small[:, 2, :]).then_inc(s["tot_ready"], 1)
            dve.wait_ge(s["slot_psum"], 1)
            link(nc.vector.tensor_copy(slot[:, 0:512], ps[:, 6, :]))
            link(nc.vector.tensor_copy(slot[:, 512:SL * P], ps[:, 7, 0:SL * P - 512]))
            link(nc.vector.tensor_scalar(rs[:, 3, 0:1], iota_col[:, :], float(REST), None, ALU.is_lt))
            link(nc.vector.tensor_scalar(rs[:, 3, 1:2], rs[:, 3, 0:1], -1.0, None, ALU.add))
            link(nc.vector.tensor_scalar(slot[:, FULLT:FULLT + 1], slot[:, FULLT:FULLT + 1], rs[:, 3, 0:1], rs[:, 3, 1:2], ALU.mult, ALU.add))
            link(nc.vector.memset(slot[:, FULLT + 1:SL * P], -1.0))
            dve.wait_ge(s["te_copied"], 4)
            link(nc.vector.tensor_copy(src_col[:, :], idx[:, :]))
            link(nc.vector.tensor_scalar(src_col[:, FULLT:FULLT + 1], src_col[:, FULLT:FULLT + 1], rs[:, 3, 0:1], rs[:, 3, 1:2], ALU.mult, ALU.add))
            link(nc.vector.memset(src_col[:, FULLT + 1:SL * P], -1.0))
            link(nc.vector.tensor_scalar(rs[:, 3, 2:3], iota_col[:, :], float(N), None, ALU.add))
            link(nc.vector.tensor_scalar(spare[:, :], src_col[:, :], -1.0, rs[:, 3, 2:3], ALU.mult, ALU.add))
            dve.wait_ge(s["te_copied"], 6)
            dve.wait_ge(s["w_loads"], 16 * 28)
            b0, b1, b2 = bpart[:, 0], bpart[:, 1], bpart[:, 2]
            link(nc.vector.tensor_copy(b0, bias3[:, :, :]))
            link(nc.vector.tensor_tensor(bres[:, 0], bias3[:, :, :], b0, ALU.subtract))
            link(nc.vector.tensor_copy(b1, bres[:, 0]))
            link(nc.vector.tensor_tensor(bres[:, 1], bres[:, 0], b1, ALU.subtract))
            link(nc.vector.tensor_copy(b2, bres[:, 1]))
            for r in range(3):
                link(nc.vector.tensor_scalar(rs[0:3, 2, r:r + 1], iota_col[0:3, :], float(r), None, ALU.is_equal))
            link(nc.vector.tensor_scalar(b0, b0, rs[0:3, 2, 0:1], None, ALU.mult))
            link(nc.vector.scalar_tensor_tensor(b0, b1, rs[0:3, 2, 1:2], b0, ALU.mult, ALU.add))
            link(nc.vector.scalar_tensor_tensor(b0, b2, rs[0:3, 2, 2:3], b0, ALU.mult, ALU.add))
            for r in range(4):
                then_chain(nc.vector.tensor_copy(brow[:, :, r, :], b0))
            then_chain(nc.vector.tensor_scalar(cap_bo1[:, :], bo1c[:, :], -1.0, CAP, ALU.mult, ALU.add))
            nc.vector.tensor_scalar(bo1_log2[:, :], bo1c[:, :], -LOG2, None, ALU.add).then_inc(s["bias_ready"], 1)
            dve.wait_ge(s["wt_psum"], 1)
            nc.vector.tensor_copy(wT[:, :, :].rearrange("p a f -> p (a f)"), ps[:, 0, :]).then_inc(s["wt_ready"], 1)
            for g in range(NG):
                dve.wait_ge(s["h_psum"], g + 1)
                nc.vector.tensor_copy(rowsD[:, g * GW:(g + 1) * GW, :],
                                      wide(3)[:, 0:GW * F].rearrange("p (w f) -> p w f", f=F)).then_inc(s["h_sb"], 1)
            dve.wait_ge(s["zero_rows"], 16 * (1 + C))

            dve_regs = [dve.alloc_register(f"dve_first{j}") for j in range(4)]

            def make_hot(l, v, q):
                if later(q, 2):
                    dve.wait_ge(agg_rdy[l], q - 1)
                for j in range(4):
                    ins = nc.vector.tensor_scalar(hot[:, v % 2, j, :], iota_row[:, :], slot[:, bass.ds(4 * q + j, 1)],
                                                  None, ALU.is_equal)
                ins.then_inc(hot_rdy[l], 1)

            def same_source(k, v, q):
                dve.wait_ge(s[f"src_loaded{v % 2}"], src_loads(k, v))
                if later(q, 2):
                    dve.wait_ge(s["sums_ready"], q - 1)
                for j in range(4):
                    ins = nc.vector.scalar_tensor_tensor(
                        hot[:, v % 2, j, :], src_row[:, v % 2, j * P:(j + 1) * P], src_col[:, bass.ds(4 * q + j, 1)],
                        tri_le[:, :], ALU.is_equal, ALU.mult, accum_out=rank[:, v % 2, j:j + 1])
                ins.then_inc(s["hot_ready"], 1)
                dve.wait_ge(s["hot_ready"], q + 1)
                link_q(nc.vector.scalar_tensor_tensor(other[:, v % 2, :], rank[:, v % 2, :], 1.0,
                                                      spare[:, bass.ds(4 * q, 4)], ALU.not_equal, ALU.mult), q)
                if later(q, 2):
                    for j in range(C):
                        dve.wait_ge(added[j], 16 * (q - 1))
                nc.vector.tensor_tensor(add_idx[:, v % 2, :], other[:, v % 2, :], src_col[:, bass.ds(4 * q, 4)],
                                        ALU.add).then_inc(s["add_idx_ready"], 1)

            def link_q(ins, q):
                ins.then_inc(s["other_ready"], 1)
                dve.wait_ge(s["other_ready"], q + 1)

            def src_loads(k, v):
                return 16 * (4 * k + v // 2 + 1)

            def accumulate(l, v, q):
                firsts = load_firsts(dve, dve_regs, q)
                dve.wait_ge(agg_rdy[l], q + 1)
                for j in range(4):
                    if j or later(q, 1):
                        dve.wait_ge(acc_dn[l], 4 * q + j)
                    a = aggT[:, bass.ds(firsts[j], P)]
                    nc.vector.tensor_tensor(a, ps[:, 5 + v % 2, j * P:(j + 1) * P], a, ALU.add).then_inc(acc_dn[l], 1)

            def step0(i, u):
                c = back(i, u, 1)
                if c:
                    _, v, q = c
                    dve.wait_ge(s["soft_done"], 3 * q + 3)
                    if later(q, 2):
                        dve.wait_ge(s["z2_ready"], q - 1)
                    nc.vector.scalar_tensor_tensor(act_s[:, v % 2, :], ps[:, 1 + v % 2, :], -LOG2, soft[:, v % 2, :],
                                                   ALU.add, ALU.max).then_inc(s["ssp_done"], 1)
                c = back(i, u, 2)
                if c:
                    same_source(*c)
                c = back(i, u, 2)
                if c:
                    k, v, q = c
                    dve.wait_ge(s["z2_ready"], q + 1)
                    dve.wait_ge(gathered[v], 64 * (k + 1))
                    for j in range(4):
                        xj = hg[:, v, j, :]
                        ins = nc.vector.scalar_tensor_tensor(xj, ps[:, 3 + v % 2, j * P:(j + 1) * P],
                                                             weight[:, bass.ds(4 * q + j, 1)], xj, ALU.mult, ALU.mult)
                    ins.then_inc(s["x_ready"], 1)

            edge_steps(dve, 2, step0)

            def step12(l):
                def step(i, u):
                    c = back(i, u, 0)
                    if c:
                        make_hot(l, c[1], c[2])
                    c = back(i, u, 1)
                    if c:
                        accumulate(l, c[1], c[2])
                return step

            def metadata():
                dve.wait_ge(s["md_sb"], 1)
                link(nc.vector.tensor_copy(endD[:, 1:NW + 1], metaD[:, :, 1]))
                link(nc.vector.tensor_scalar(cntD[:, 0, :], endD[:, 1:NW + 1], 0.0, NO_NODE, ALU.is_equal, ALU.mult))
                link(nc.vector.tensor_tensor(cntD[:, 1, :], cntD[:, 0, :], metaD[:, :, 0], ALU.add))
                nc.vector.tensor_copy(node_id[:, :], cntD[:, 1, :]).then_inc(s["ids_ready"], 1)
                dve.wait_ge(s["cnt_psum"], 1)
                link(nc.vector.tensor_tensor(cntD[:, 0, :], endD[:, 1:NW + 1], ps[:, 7, 256:256 + NW], ALU.subtract))
                link(nc.vector.tensor_scalar(cntD[:, 0, :], cntD[:, 0, :], 1.0, None, ALU.max))
                nc.vector.reciprocal(cntD[:, 2, :], cntD[:, 0, :]).then_inc(s["tot_ready"], 1)

            def norm_stats(n, yw):
                for j in range(GW):
                    ins = nc.vector.bn_stats(stats[:, j, :], yw[:, j, :])
                link(ins)
                for j in range(GW):
                    ins = nc.vector.bn_aggr(mv[:, j, :], stats[:, j, :])
                ins.then_inc(n["var_done"], 1)

            def norm_apply(n, h, yw, dest):
                dve.wait_ge(n["rstd"], h + 1)
                r = rs[:, 1, :]
                link(nc.vector.tensor_tensor(rs[:, 2, :], r, r, ALU.mult))
                link(nc.vector.scalar_tensor_tensor(rs[:, 3, :], mv[:, :, 1], EPS, rs[:, 2, :], ALU.add, ALU.mult))
                link(nc.vector.tensor_scalar(rs[:, 3, :], rs[:, 3, :], -0.5, 1.5, ALU.mult, ALU.add))
                link(nc.vector.tensor_tensor(rs[:, 2, :], r, rs[:, 3, :], ALU.mult))
                for j in range(GW):
                    ins = nc.vector.tensor_scalar(dest[:, j, :], yw[:, j, :], mv[:, j, 0:1], rs[:, 2, j:j + 1],
                                                  ALU.subtract, ALU.mult)
                ins.then_inc(n["y_done"], 1)
                dve.wait_ge(n["y_done"], h + 1)

            def node_phase(l):
                n = node[l]
                for g in range(NG + 1):
                    if l == 0 and g < NG:
                        dve.wait_ge(n["nt_soft"], g + 1)
                        if g >= 2:
                            dve.wait_ge(n["out_psum"], g - 1)
                        nc.vector.scalar_tensor_tensor(nS[:, g % 2, :], wide(2)[:, 0:GW * F], bo1_log2[:, :], nT[:, :],
                                                       ALU.add, ALU.max).then_inc(n["ssp"], 1)
                    if l == 0 and g >= 1:
                        h = g - 1
                        xw = x_sb[:, h * GW:(h + 1) * GW, :]
                        yw = yv[:, h % 2]
                        dve.wait_ge(n["out_psum"], h + 1)
                        ins = nc.vector.tensor_tensor(yw, wide(0)[:, 0:GW * F].rearrange("p (w f) -> p w f", f=F), xw, ALU.add)
                        ins.then_inc(n["sum_done"], 1)
                        dve.wait_ge(n["sum_done"], h + 1)
                        norm_stats(n, yw)
                        norm_apply(n, h, yw, xw)
                    if l >= 1 and g < NG:
                        h = g
                        xw = x_sb[:, h * GW:(h + 1) * GW, :]
                        yw = yv[:, h % 2]
                        rw = root[:, h * GW * F:(h + 1) * GW * F].rearrange("p (w f) -> p w f", f=F)
                        dve.wait_ge(n[f"rows_loaded{h % 2}"], 16 * (h // 2 + 1))
                        if h >= 2:
                            dve.wait_ge(n[f"stored{h % 2}"], 16 * (h // 2))
                            if l == 1:
                                dve.wait_ge(n["yt_psum"], h - 1)
                        nc.vector.tensor_tensor(yw, rowsN[:, h % 2], rw, ALU.add).then_inc(n["relu_in"], 1)
                        dve.wait_ge(n["relu_in"], h + 1)
                        if l == 1:
                            nc.vector.tensor_scalar(yw, yw, 0.0, None, ALU.max).then_inc(n["y_done"], 1)
                        else:
                            link(nc.vector.scalar_tensor_tensor(yw, yw, 0.0, xw, ALU.max, ALU.add))
                            norm_stats(n, yw)
                            norm_apply(n, h, yw, yw)

            def clear_agg(l):
                dve.wait_ge(node[l]["rows_psum" if l else "agg_psum"], NG)
                nc.vector.memset(aggT[:, :], 0.0).then_inc(agg_clear[l + 1], 1)
                dve.wait_ge(agg_clear[l + 1], 1)

            nc.vector.memset(meta_row[:, :], 0.0).then_inc(s["zero_meta"], 1)
            node_phase(0)
            clear_agg(0)
            edge_steps(dve, 1, step12(1))
            metadata()
            clear_agg(1)
            node_phase(1)
            edge_steps(dve, 1, step12(2))
            node_phase(2)

        @block.tensor
        def _(pe):
            def bias(out_ap, n):
                c = out_ap.shape[-1]
                for b in range(0, c, 512):
                    w = min(512, c - b)
                    nc.tensor.matmul(out_ap[:, b:b + w], ones3[:, :],
                                     brow[:, n, :, :].rearrange("r a f -> r (a f)")[:, 0:w],
                                     start=True, stop=False, skip_group_check=True)

            pe.wait_ge(s["te_ready"], 1)
            for n, v in enumerate((start_te, id_te, end_te, src_te, ew_te, dst_te)):
                if n >= 2:
                    pe.wait_ge(s["te_copied"], n - 1)
                for k in range(SL):
                    ins = nc.tensor.transpose(wide(n % 2)[:, k * P:(k + 1) * P], v[:, k * P:(k + 1) * P], ident[:, :])
                ins.then_inc(s["te_psum"], 1)
                if n == 0:
                    nc.tensor.matmul(ps[:, 6, 0:SL], tri_strict[:, :], small[:, 0, :], start=True, stop=False)
                    nc.tensor.matmul(ps[:, 6, 0:SL], ones[:, :], small[:, 1, :], start=False, stop=True).then_inc(s["pref_ready"], 1)
            pe.wait_ge(s["tot_ready"], 1)
            for k in range(SL):
                ins = nc.tensor.transpose(wide(2)[0:1, k * P:(k + 1) * P], small[:, 0, k:k + 1], ident[:, :])
            ins.then_inc(s["first_psum"], 1)
            pe.wait_ge(s["te_copied"], 1)
            nc.tensor.matmul(ps[:, 6, :], tri_incl0[:, :], start_te[:, 0:512], start=True, stop=True)
            nc.tensor.matmul(ps[:, 7, 0:SL * P - 512], tri_incl0[:, :], start_te[:, 512:SL * P], start=True, stop=True).then_inc(s["slot_psum"], 1)
            pe.wait_ge(s["te_copied"], 6)
            pe.wait_ge(s["w_loads"], 16 * 28)
            for k in range(4):
                ins = nc.tensor.transpose(ps[:, 0, k * P:(k + 1) * P], wraw[:, k, :], ident[:, :])
            ins.then_inc(s["wt_psum"], 1)
            pe.wait_ge(s["bias_ready"], 1)
            pe.wait_ge(s["first_ready"], 1)
            for g in range(NG):
                if g >= 1:
                    pe.wait_ge(s["xt_sb"], g)
                for j in range(GW):
                    ins = nc.tensor.transpose(wide(2)[:, j * P:(j + 1) * P], x_sb[:, g * GW + j, :], ident[:, :])
                ins.then_inc(s["xt_psum"], 1)
                pe.wait_ge(s["xt_sb"], g + 1)
                if g >= 1:
                    pe.wait_ge(s["h_sb"], g)
                bias(wide(3)[:, 0:GW * F], 0)
                for j in range(GW):
                    ins = nc.tensor.matmul(wide(3)[:, j * F:(j + 1) * F], xT[:, j * P:(j + 1) * P], w_in[:, :],
                                           start=False, stop=True, skip_group_check=True)
                ins.then_inc(s["h_psum"], 1)
            pe.wait_ge(s["h_sb"], NG)
            pe.wait_ge(s["wt_ready"], 1)

            def step0(i, u):
                c = back(i, u, 0)
                if c:
                    k, v, q = c
                    pe.wait_ge(f_loaded[v], 16 * (k + 1))
                    if later(q, 1):
                        pe.wait_ge(s["ft_copied"], q)
                    for j in range(4):
                        ins = nc.tensor.transpose(ps[0:K, 0, j * P:(j + 1) * P], f_sb[:, v, j * K:(j + 1) * K], ident[:, :])
                    ins.then_inc(s["ft_ready"], 1)
                c = back(i, u, 1)
                if c:
                    _, v, q = c
                    pe.wait_ge(s["ft_copied"], q + 1)
                    if later(q, 2):
                        pe.wait_ge(s["ssp_done"], q - 1)
                    nc.tensor.matmul(ps[:, 1 + v % 2, :], wf1[:, :], fT[:, v % 2, :], start=True, stop=True).then_inc(s["z1_ready"], 1)
                c = back(i, u, 2)
                if c:
                    _, v, q = c
                    pe.wait_ge(s["ssp_done"], q + 1)
                    if later(q, 2):
                        pe.wait_ge(s["x_ready"], q - 1)
                    z = ps[:, 3 + v % 2, :]
                    bias(z, 1)
                    for j in range(4):
                        ins = nc.tensor.matmul(z[:, j * F:(j + 1) * F], act_s[:, v % 2, j * P:(j + 1) * P], wf2[:, :],
                                               start=False, stop=True, skip_group_check=True)
                    ins.then_inc(s["z2_ready"], 1)
                c = back(i, u, 3)
                if c:
                    _, v, q = c
                    pe.wait_ge(s["hot_ready"], q + 1)
                    pe.wait_ge(s["x_ready"], q + 1)
                    if later(q, 2):
                        pe.wait_ge(s["sums_sb"], q - 1)
                    for j in range(4):
                        ins = nc.tensor.matmul(ps[:, 5 + v % 2, j * P:(j + 1) * P], hot[:, v % 2, j, :], hg[:, v, j, :],
                                               start=True, stop=True)
                    ins.then_inc(s["sums_ready"], 1)

            edge_steps(pe, 3, step0)

            def step12(l):
                def step(i, u):
                    q = i * U + u
                    pe.wait_ge(hot_rdy[l], q + 1)
                    if l == 1:
                        pe.wait_ge(s["meta_staged"], q + 1)
                        if later(q, 1):
                            pe.wait_ge(s["meta_copied"], 4 * q)
                        for j in range(4):
                            nc.tensor.matmul(ps[0:2, 7, j * P:(j + 1) * P], meta_stage[:, u % 2, j, :], hot[:, u % 2, j, :],
                                             start=True, stop=True)
                    if later(q, 2):
                        pe.wait_ge(acc_dn[l], 4 * (q - 1))
                    pe.wait_ge(gathered[u], 64 * (NI * l + i + 1))
                    for j in range(4):
                        ins = nc.tensor.matmul(ps[:, 5 + u % 2, j * P:(j + 1) * P], hg[:, u, j, :], hot[:, u % 2, j, :],
                                               start=True, stop=True)
                    ins.then_inc(agg_rdy[l], 1)
                return step

            def metadata():
                pe.wait_ge(s["meta_copied"], TP)
                for w in range(NW):
                    ins = nc.tensor.transpose(ps[:, 7, 2 * w:2 * w + 2], meta_row[:, w * P:(w + 1) * P], ident[0:2, 0:2])
                ins.then_inc(s["md_psum"], 1)
                pe.wait_ge(s["ids_ready"], 1)
                nc.tensor.matmul(ps[:, 7, 256:256 + NW], shift[:, :], endD[:, 1:NW + 1], start=True, stop=False)
                nc.tensor.matmul(ps[:, 7, 256:256 + NW], corner[:, :], endD[:, 0:NW], start=False, stop=True).then_inc(s["cnt_psum"], 1)

            first_w = [None, wT[:, 0, :], wT[:, 2, :]]

            def node_phase(l):
                n = node[l]
                if l:
                    pe.wait_ge(acc_dn[l], TP)
                if l == 1:
                    metadata()
                for g in range(NG if l else 0):
                    if g >= 2:
                        pe.wait_ge(n["rows_sb"], g - 1)
                    for j in range(GW):
                        w = g * GW + j
                        ins = nc.tensor.matmul(wide(g % 2)[:, j * F:(j + 1) * F], aggT[:, w * P:(w + 1) * P], first_w[l],
                                               start=True, stop=True)
                    ins.then_inc(n["rows_psum"], 1)
                if l:
                    pe.wait_ge(n["rows_sb"], NG)
                for g in range(NG + 2):
                    if l == 0 and g < NG:
                        pe.wait_ge(n["rows_summed"], 3 * (g + 1))
                        if g >= 3:
                            pe.wait_ge(n["yt_sb"], g - 2)
                        for j in range(GW):
                            ins = nc.tensor.transpose(wide(1)[:, j * P:(j + 1) * P], agg_n[:, g % 2, j, :], ident[:, :])
                        ins.then_inc(n["agg_psum"], 1)
                        pe.wait_ge(n["agg_sb"], g + 1)
                        if g >= 1:
                            pe.wait_ge(n["ssp"], g)
                        nc.tensor.matmul(wide(2)[:, 0:512], wo1[:, :], gT[:, 0:512], start=True, stop=True)
                        nc.tensor.matmul(wide(2)[:, 512:GW * F], wo1[:, :], gT[:, 512:GW * F], start=True, stop=True).then_inc(n["nt_psum"], 1)
                    h = g - 1
                    if l == 0 and 0 <= h < NG:
                        pe.wait_ge(n["ssp"], h + 1)
                        if h >= 1:
                            pe.wait_ge(n["sum_done"], h)
                        bias(wide(0)[:, 0:GW * F], 2)
                        for j in range(GW):
                            ins = nc.tensor.matmul(wide(0)[:, j * F:(j + 1) * F], nS[:, h % 2, j * P:(j + 1) * P], wo2[:, :],
                                                   start=False, stop=True, skip_group_check=True)
                        ins.then_inc(n["out_psum"], 1)
                    h = g - 2
                    if l < 2 and h >= 0:
                        pe.wait_ge(n["y_done"], h + 1)
                        if h >= 1:
                            pe.wait_ge(n["yt_sb"], h)
                        for j in range(GW):
                            y = x_sb[:, h * GW + j, :] if l == 0 else yv[:, h % 2, j, :]
                            ins = nc.tensor.transpose(wide(1)[:, j * P:(j + 1) * P], y, ident[:, :])
                        ins.then_inc(n["yt_psum"], 1)
                        pe.wait_ge(n["yt_sb"], h + 1)
                        if h >= 1:
                            pe.wait_ge(n["root_done"], h)
                        bias(wide(3)[:, 0:GW * F], 3 + l)
                        for j in range(GW):
                            ins = nc.tensor.matmul(wide(3)[:, j * F:(j + 1) * F], yT[:, j, :], wT[:, 1 + 2 * l, :],
                                                   start=False, stop=True, skip_group_check=True)
                        ins.then_inc(n["root_psum"], 1)
                if l < 2:
                    pe.wait_ge(n["root_done"], NG)

            node_phase(0)
            edge_steps(pe, 0, step12(1))
            node_phase(1)
            edge_steps(pe, 0, step12(2))
            node_phase(2)


_INS = ["x", "src", "dst", "edge_attr_20", "edge_weight"] + [f"L0_gnn_{n}" for n in (
    "W_in", "b_in", "Wf1", "bf1", "Wf2", "bf2", "Wo1", "bo1", "Wo2", "bo2")] + [
    f"L1_gnn_{n}" for n in ("Wl1", "bl1", "Wr1", "Wl2", "bl2", "Wr2")]


def kernel(**inputs):
    import concourse.bacc as bacc
    from concourse.bass_utils import run_bass_kernel_spmd

    nc = bacc.Bacc("TRN2", target_bir_lowering=False, num_devices=1)
    arrays, args = {}, []
    for name in _INS:
        a = np.ascontiguousarray(inputs[name])
        arrays[f"in_{name}"] = a
        args.append(nc.dram_tensor(f"in_{name}", a.shape, mybir.dt.from_np(a.dtype), kind="ExternalInput").ap())
    shape = inputs["x"].shape
    args.append(nc.dram_tensor("out_0", shape, F32, kind="ExternalOutput").ap())
    gnn_program(nc, *args)
    r = run_bass_kernel_spmd(nc, [arrays], core_ids=[0])
    return r.results[0]["out_0"]
```

```python
from contextlib import ExitStack

import numpy as np

import concourse.bass as bass
from concourse import mybir

F32 = mybir.dt.float32
BF16 = mybir.dt.bfloat16
I32 = mybir.dt.int32
ALU = mybir.AluOpType
ACT = mybir.ActivationFunctionType
AX = mybir.AxisListType

P = 128
LOG2 = float(np.log(2.0))
CAP = 20.0
EPS = 1e-5


def gnn_program(nc, x, src, dst, edge_attr, edge_weight, W_in, b_in, Wf1, bf1, Wf2, bf2, Wo1, bo1,
                Wo2, bo2, Wl1, bl1, Wr1, Wl2, bl2, Wr2, out):
    N, F = x.shape
    E, K = edge_attr.shape
    assert F == P
    T = -(-E // P)
    U = 8
    Q = -(-T // (4 * U)) * U
    NI = Q // U
    TP = 4 * Q
    NW = -(-N // P)
    GW = 7
    NG = NW // GW
    NP = NW * P
    AW = NP + P
    SL = -(-T // P)
    TC = SL * P
    FULLT = E // P
    REST = E - FULLT * P
    FULLQ = E // (4 * P)
    RESTQ = E - FULLQ * 4 * P
    C = 4
    assert NW == NG * GW and N % P and SL == GW and TC >= TP and REST and FULLQ == Q - 1 and C == 4

    def internal(name, shape, dt=F32):
        return nc.dram_tensor(name, shape, dt, kind="Internal").ap()

    h_dram = internal("h_dram", [AW, F])
    x1_dram = internal("x1_dram", [NP, F])
    h1_dram = internal("h1_dram", [NP, F])
    rel_dram = internal("rel_dram", [TC * P], BF16)
    acc_dram = [[internal(f"acc_dram{l}_{j}", [AW, F]) for j in range(2 * C)] for l in range(3)]

    with ExitStack() as ctx:
        def sb(name, shape, dt=F32):
            return ctx.enter_context(nc.sbuf_tensor(name, shape, dt))

        def sem(name):
            return ctx.enter_context(nc.semaphore(name))

        x_sb = sb("x_sb", [P, NW, F])
        root = sb("root", [P, NP])
        aggT = sb("aggT", [P, AW])
        src_idx = sb("src_idx", [P, TC], I32)
        dst_idx = sb("dst_idx", [P, TC], I32)
        weight = sb("weight", [P, TC])
        src_col = sb("src_col", [P, TC])
        dst_col = sb("dst_col", [P, TC])
        spare = sb("spare", [P, TC])
        slot = sb("slot", [P, TC])
        dst_hi = sb("dst_hi", [P, TC])
        dst_lo = sb("dst_lo", [P, TC])
        first_row = sb("first_row", [1, TC], I32)
        ident = sb("ident", [P, P])
        iota_row = sb("iota_row", [P, P])
        iota_col = sb("iota_col", [P, 1])
        tri_le = sb("tri_le", [P, P])
        ones = sb("ones", [P, P])
        wraw = sb("wraw", [P, 4, F])
        wT = sb("wT", [P, 4, F])
        w_in = sb("w_in", [P, F])
        wf1 = sb("wf1", [K + 1, F])
        wf2 = sb("wf2", [P, F])
        wo1 = sb("wo1", [P, F])
        wo2 = sb("wo2", [P, F])
        bo1c = sb("bo1c", [P, 1])
        cap_bo1 = sb("cap_bo1", [P, 1])
        bo1_log2 = sb("bo1_log2", [P, 1])
        cap_col = sb("cap_col", [P, 1])
        half_col = sb("half_col", [P, 1])
        eps_col = sb("eps_col", [P, 1])
        tail_col = sb("tail_col", [P, 3])
        NB = 5
        brow = sb("brow", [3, NB, 4, F], BF16)
        pick = sb("pick", [3, 3])
        ones3 = sb("ones3", [3, P], BF16)
        flag = sb("flag", [1, 1], I32)
        flag_f = sb("flag_f", [P, 4])
        prev_i = sb("prev_i", [P, SL], I32)
        prev_f = sb("prev_f", [P, SL])
        f_sb = sb("f_sb", [P, U, 4 * K])
        fT = sb("fT", [K + 1, 2, 4 * P])
        act_buf = sb("act_buf", [P, 4, 4 * P])
        soft, act_s = act_buf[:, 0:2, :], act_buf[:, 2:4, :]
        ring = sb("ring", [P, U, 4, F])
        spread = sb("spread", [P, 2, 4 * P])
        rows = sb("rows", [P, 4, 4, F])
        hot = sb("hot", [P, 4, 4, P])
        key_row = sb("key_row", [P, 4, 4 * P], I32)
        rel_row = sb("rel_row", [P, 4, 4 * P], BF16)
        rank = sb("rank", [P, 2, 4])
        other = sb("other", [P, 2, 4])
        add_idx = sb("add_idx", [P, 4, 4], I32)
        sums = sb("sums", [P, 4, 4, F])
        idx_stage = sb("idx_stage", [P, 2, 16], I32)
        lo_hot = sb("lo_hot", [P, 2, 4, P], BF16)
        hi_hot = sb("hi_hot", [P, 2, 4, NW], BF16)
        yv = sb("yv", [P, 2, GW, F])
        stats = sb("stats", [P, NW, 6])
        mv = sb("mv", [P, NW, 2])
        rs = sb("rs", [P, 4, NW])
        rcnt = sb("rcnt", [P, 2, NW])
        flat = ring[:, :, :, :].rearrange("p u j f -> p (u j f)")
        yT = rows[:, :, :, :].rearrange("p u j f -> p (u j f)")[:, 0:GW * F].rearrange("p (w f) -> p w f", f=F)
        gT = sums[:, :, :, :].rearrange("p b j f -> p (b j f)")[:, 0:GW * F]
        nS = act_buf[:, :, :].rearrange("p b c -> p (b c)")[:, 0:2 * GW * F].rearrange("p (b c) -> p b c", b=2)
        def copies(l):
            return [v[:, 0:C * GW * F].rearrange("p (k w f) -> p k w f", k=C, f=F) for v in (flat, aggT, root)[:2 if l else 3]]

        nT = aggT[:, 4 * GW * F:5 * GW * F]
        def te(v):
            return v.rearrange("p (s e) -> p s e", e=P)
        dst_i, src_i, ew_te, dst_te, src_te, rel_te, diff = (root[:, k * TC:(k + 1) * TC] for k in range(7))
        dst_i, src_i = dst_i.bitcast(I32), src_i.bitcast(I32)
        valid, edge_no = (nS[:, k, :] for k in range(2))
        viol = yv[:, 0].rearrange("p w f -> p (w f)")
        rel_bf = yv[:, 1].rearrange("p w f -> p (w f)")[:, 0:TC // 2].bitcast(BF16)
        xT = flat[:, 0:GW * P]
        h_places = [v[:, k * GW * F:(k + 1) * GW * F] for v in (
            rows[:, :, :, :].rearrange("p u j f -> p (u j f)"), hot[:, :, :, :].rearrange("p u j f -> p (u j f)"),
            sums[:, :, :, :].rearrange("p b j f -> p (b j f)"), key_row[:, :, :].rearrange("p u e -> p (u e)").bitcast(F32))
            for k in range(2)][0:NG]
        bias3 = flat[0:3, 1024:1024 + NB * F].rearrange("r (n f) -> r n f", f=F)
        bres = [flat[0:3, 1664 + k * NB * F:1664 + (k + 1) * NB * F].rearrange("r (n f) -> r n f", f=F) for k in range(2)]
        bpart = [flat[0:3, 2944 + k * 320:2944 + (k + 1) * 320].bitcast(BF16).rearrange("r (n f) -> r n f", f=F) for k in range(3)]

        ps = ctx.enter_context(nc.psum_tensor("ps", [P, 8, 512], F32))

        def wide(k):
            return ps[:, 2 * k:2 * k + 2, :].rearrange("p b c -> p (b c)")

        def windows(v):
            return v.rearrange("p (w f) -> p w f", f=F)

        s = {n: sem(n) for n in """te_loads w_loads x_pad pads consts chainp chainv chaina zeroed zero_stored
            te_ready te_psum te_sb flag_psum flag_ready first_psum first_ready rel_sb rel_stored tables
            wt_psum wt_sb bias_ready xt_psum xt_sb h_psum h_sb h_stored
            key_loaded0 key_loaded1 rel_loaded0 rel_loaded1 f_rest ft_ready ft_copied z1_ready soft_done ssp_done
            z2_ready spread_ready rows_psum rows_sb x_ready same_ready other_ready add_idx_ready
            sums_ready sums_sb adds_begun quads_begun loads_begun idx_staged spare_ready
            hist_ready hist_used cnt_ready hot_ready1 hot_ready2 agg_ready1 agg_ready2 acc_done1 acc_done2
            agg_clear1 agg_clear2""".split()}
        x_loaded = [sem(f"x_loaded{g}") for g in range(NG)]
        f_loaded = [sem(f"f_loaded{u}") for u in range(U)]
        arrived = [sem(f"arrived{u}") for u in range(U)]
        windows_loaded = [sem(f"windows_loaded{u}") for u in range(U)]
        added = [[sem(f"added{b}_{j}") for j in range(C)] for b in range(2)]
        of_layers = {"stored0 stored1 copies_loaded0 copies_loaded1 copies_loaded2 pairs_summed copies_summed agg_sb": (0, 1, 2),
                     "nt_psum nt_soft ssp out_psum sum_done": (0,),
                     "var_done rstd": (0, 2),
                     "scale_done out_done0 out_done1": (2,),
                     "rows_psum row_done": (1, 2),
                     "y_done yt_psum yt_sb root_psum root_done": (0, 1)}
        node = [{n: sem(f"{n}_{l}") for ns, ls in of_layers.items() if l in ls for n in ns.split()} for l in range(3)]

        block = ctx.enter_context(nc.Block())

        STAGED = 2 * NI + 1

        def edge_steps(eng, skew, step):
            peeled = 1 if skew <= 4 else 2
            for i in range(peeled):
                for u in range(U):
                    step(i, u)
            with eng.Fori(peeled, NI) as i:
                for u in range(U):
                    step(i, u)
            for u in range(skew):
                step(NI, u)

        def back(i, u, k):
            d = u - k
            i, u = i + d // U, d % U
            if isinstance(i, int) and not 0 <= i < NI:
                return None
            return i, u, i * U + u

        def later(q, n):
            return not isinstance(q, int) or q >= n

        def wait_added(eng, k, v, q, base, ago, accumulators=range(C)):
            if base or later(q, 2 + 2 * ago):
                for j in accumulators:
                    eng.wait_ge(added[v % 2][j], 16 * (base // 2 + k * (U // 2) + v // 2 - ago))

        def load_firsts(eng, regs, q):
            eng.load(regs, first_row[0:1, bass.ds(4 * q, 4)])
            return [eng.snap(r, min_val=0, max_val=N - 1) for r in regs]

        def two_ways(eng, ordered, general, chain=(0,)):
            eng.wait_ge(s["flag_ready"], 1)
            way = eng.alloc_register("way")
            eng.load([way], flag[0:1, 0:1])
            with eng.If_eq(way, 1):
                before = chain[0]
                ordered()
            with eng.Else():
                if chain[0] != before:
                    chain[0] = before
                general()

        def normalise(eng, h):
            for w in range(h * GW, (h + 1) * GW):
                y = root[:, w * F:(w + 1) * F]
                ins = eng.tensor_scalar(y, y, mv[:, w, 0:1], rs[:, 2, w:w + 1], ALU.subtract, ALU.mult)
            return ins

        def all_stored(eng, n, extra=0):
            eng.wait_ge(n["stored0"], 16 * (NG - NG // 2 + extra))
            eng.wait_ge(n["stored1"], 16 * (NG // 2))

        @block.sync
        def _(sp):
            whole = (SL - 1) * P
            part = FULLT - whole
            sp.wait_ge(s["x_pad"], 1)
            sp.wait_ge(s["pads"], 1)

            def load_x(g):
                w0, w1 = g * GW, min((g + 1) * GW, NW - 1)
                sp.dma_start(x_sb[:, w0:w1, :], x[w0 * P:w1 * P, :].rearrange("(w p) f -> p w f", p=P)).then_inc(x_loaded[g], 16)
                if w1 < (g + 1) * GW:
                    sp.dma_start(x_sb[0:N - w1 * P, w1, :], x[w1 * P:N, :]).then_inc(x_loaded[g], 16)

            def load_te(v, d):
                t3 = te(v)
                sp.dma_start(t3[:, 0:SL - 1, :], d[0:whole * P].rearrange("(s t e) -> t s e", t=P, e=P)).then_inc(s["te_loads"], 16)
                sp.dma_start(t3[0:part, SL - 1, :], d[whole * P:FULLT * P].rearrange("(t e) -> t e", e=P)).then_inc(s["te_loads"], 16)
                sp.dma_start(t3[part:part + 1, SL - 1, 0:REST], d[FULLT * P:E].rearrange("(t e) -> t e", t=1)).then_inc(s["te_loads"], 16)

            load_x(0)
            sp.dma_start(w_in[:, :], W_in).then_inc(s["w_loads"], 16)
            for n, b in enumerate((b_in, bf2, bo2, bl1, bl2)):
                sp.dma_start(bias3[:, n, :], b.rearrange("(a f) -> a f", a=1).broadcast_to([3, F])).then_inc(s["w_loads"], 16)
            load_te(dst_i, dst)
            d2 = dst[0:FULLT * P].rearrange("(t e) -> t e", e=P)[:, P - 1:P]
            sp.dma_start(prev_i[1:P, 0:1], d2[0:P - 1, :], allow_slow_non_contiguous=True).then_inc(s["te_loads"], 16)
            for sl in range(1, SL):
                n = min(P, FULLT - (sl * P - 1))
                sp.dma_start(prev_i[0:n, sl:sl + 1], d2[sl * P - 1:sl * P - 1 + n, :],
                             allow_slow_non_contiguous=True).then_inc(s["te_loads"], 16)
            load_te(src_i, src)
            load_te(ew_te, edge_weight)
            for g in range(1, NG):
                load_x(g)
            for t, d in ((wf2, Wf2), (wo1, Wo1), (wo2, Wo2), (wraw[:, 0, :], Wl1),
                         (wraw[:, 1, :], Wr1), (wraw[:, 2, :], Wl2), (wraw[:, 3, :], Wr2), (wf1[0:K, :], Wf1)):
                sp.dma_start(t[:, :], d).then_inc(s["w_loads"], 16)
            sp.dma_start(wf1[K:K + 1, :], bf1.rearrange("(a f) -> a f", a=1)).then_inc(s["w_loads"], 16)
            sp.dma_start(bo1c[:, :], bo1.rearrange("(f a) -> f a", a=1), allow_slow_non_contiguous=True).then_inc(s["w_loads"], 16)
            sp.wait_ge(s["zeroed"], 1)
            for a in acc_dram[0][0:C]:
                sp.dma_start(a.rearrange("(p w) f -> p (w f)", p=P), aggT[:, :]).then_inc(s["zero_stored"], 16)
            sp.dma_start(h_dram[NP:AW, :], aggT[:, 0:F]).then_inc(s["zero_stored"], 16)
            sp.wait_ge(s["rel_sb"], 1)
            sp.dma_start(rel_dram.rearrange("(s t e) -> t s e", t=P, e=P), te(rel_bf)).then_inc(s["rel_stored"], 16)
            for g in range(NG):
                sp.wait_ge(s["h_sb"], g + 1)
                sp.dma_start(h_dram[g * GW * P:(g + 1) * GW * P, :].rearrange("(w p) f -> p w f", p=P),
                             windows(h_places[g])).then_inc(s["h_stored"], 16)
            for a in acc_dram[0][C:2 * C]:
                sp.dma_start(a.rearrange("(p w) f -> p (w f)", p=P), aggT[:, :]).then_inc(s["zero_stored"], 16)

            f_v = edge_attr[0:FULLQ * 4 * P, :].rearrange("(q p a) k -> p q (a k)", p=P, a=4)
            regs = [sp.alloc_register(f"sp_first{j}") for j in range(4)]

            def load_features(q, u):
                if later(q, U):
                    sp.wait_ge(s["ft_ready"], q - U + 2)
                    sp.sem_inc(s["loads_begun"], 1)
                if isinstance(q, int) and q == FULLQ - 1:
                    fp, e0 = RESTQ // 4, FULLQ * 4 * P
                    sp.dma_start(f_sb[:, u, :], f_v[:, q, :]).then_inc(s["f_rest"], 16)
                    sp.dma_start(f_sb[fp:fp + 1, u + 1, 0:(RESTQ % 4) * K],
                                 edge_attr[e0 + 4 * fp:E, :].rearrange("(p a) k -> p (a k)", p=1)).then_inc(s["f_rest"], 16)
                    sp.wait_ge(s["f_rest"], 32)
                    sp.dma_start(f_sb[0:fp, u + 1, :], edge_attr[e0:e0 + 4 * fp, :].rearrange("(p a) k -> p (a k)", a=4)).then_inc(f_loaded[u], 16)
                else:
                    sp.dma_start(f_sb[:, u:u + 2, :], f_v[:, bass.ds(q, 2), :]).then_inc(f_loaded[u], 16)

            def load_keys(q, u, keys, base=0):
                if base or later(q, 4):
                    sp.wait_ge(s["same_ready"], q + base - 2)
                    sp.sem_inc(s["loads_begun"], 1)
                n = 4 * P + RESTQ if isinstance(q, int) and q == FULLQ - 1 else 8 * P
                row = keys[bass.ds(q * 4 * P, n)].rearrange("(a e) -> a e", a=1).broadcast_to([P, n])
                dest = key_row[:, u % 4:u % 4 + 2, :].rearrange("p a e -> p (a e)")
                sp.dma_start(dest[:, 0:n], row).then_inc(s[f"key_loaded{u // 2 % 2}"], 16)

            def sp_steps(step):
                for u in range(U):
                    step(0, u)
                with sp.Fori(1, NI - 1) as i:
                    for u in range(U):
                        step(i, u)
                for u in range(U):
                    step(NI - 1, u)

            def ordered0(i, u):
                q = i * U + u
                if u % 2 == 0:
                    load_features(q, u)
                    if later(q, 4):
                        sp.wait_ge(s["spread_ready"], q - 2)
                        sp.sem_inc(s["loads_begun"], 1)
                    row = rel_dram[bass.ds(q * 4 * P, 8 * P)].rearrange("(a e) -> a e", a=1).broadcast_to([P, 8 * P])
                    sp.dma_start(rel_row[:, u % 4:u % 4 + 2, :].rearrange("p a e -> p (a e)"), row
                                 ).then_inc(s[f"rel_loaded{u // 2 % 2}"], 16)
                    load_keys(q, u, src)
                firsts = load_firsts(sp, regs, q)
                if later(q, U):
                    sp.wait_ge(s["rows_psum"], q - U + 1)
                sp.sem_inc(s["loads_begun"], 1)
                for j in range(4):
                    sp.dma_start(ring[:, u, j, :], h_dram[bass.ds(firsts[j], P), :]).then_inc(windows_loaded[u], 16)

            def general_edges(l):
                def step(i, u):
                    q = i * U + u
                    if u % 2 == 0:
                        if l == 0:
                            load_features(q, u)
                        load_keys(q, u, dst if l else src, l * Q)
                sp_steps(step)

            def store(l, h):
                n = node[l]
                w0 = h * GW
                if l == 2:
                    sp.wait_ge(n[f"out_done{h % 2}"], h // 2 + 1)
                else:
                    sp.wait_ge(n["y_done"], h + 1)
                rows_out = (x_sb[:, :, :], windows(root[:, :]), windows(root[:, :]))[l]
                if l < 2:
                    target = (x1_dram, h1_dram)[l]
                    sp.dma_start(target[w0 * P:(w0 + GW) * P, :].rearrange("(w p) f -> p w f", p=P),
                                 rows_out[:, w0:w0 + GW, :]).then_inc(n[f"stored{h % 2}"], 16)
                else:
                    full = min(GW, NW - 1 - w0)
                    sp.dma_start(out[w0 * P:(w0 + full) * P, :].rearrange("(w p) f -> p w f", p=P),
                                 rows_out[:, w0:w0 + full, :]).then_inc(n[f"stored{h % 2}"], 16)
                    if full < GW:
                        sp.dma_start(out[(NW - 1) * P:N, :], rows_out[0:N - (NW - 1) * P, w0 + full, :]).then_inc(n[f"stored{h % 2}"], 16)

            def load_copies(l, g):
                n = node[l]
                for b in range(2):
                    t, places = 2 * g + b, copies(l)
                    if t >= len(places):
                        sp.wait_ge(n["copies_summed"], t - len(places) + 1)
                    for k in range(C):
                        sp.dma_start(places[t % len(places)][:, k], acc_dram[l][C * b + k][g * GW * P:(g + 1) * GW * P, :]
                                     .rearrange("(w p) f -> p w f", p=P)).then_inc(n[f"copies_loaded{t % len(places)}"], 16)

            def node_traffic(l, summed):
                if summed:
                    for a in added[0] + added[1]:
                        sp.wait_ge(a, 16 * Q // 2 * (l + 1))
                    load_copies(l, 0)
                lead = NG if l == 2 else 3
                for g in range(1, NG + lead):
                    if summed and g < NG:
                        load_copies(l, g)
                    if g >= lead:
                        store(l, g - lead)

            def ordered():
                sp.wait_ge(s["h_stored"], 16 * NG)
                sp.wait_ge(s["zero_stored"], 16 * (2 * C + 1))
                sp.wait_ge(s["rel_stored"], 16)
                sp.wait_ge(s["first_ready"], 1)
                sp_steps(ordered0)
                node_traffic(0, True)
                node_traffic(1, False)
                node_traffic(2, False)

            def general():
                for a in acc_dram[1] + acc_dram[2]:
                    sp.dma_start(a.rearrange("(p w) f -> p (w f)", p=P), aggT[:, :]).then_inc(s["zero_stored"], 16)
                general_edges(0)
                node_traffic(0, True)
                general_edges(1)
                node_traffic(1, True)
                general_edges(2)
                node_traffic(2, True)

            two_ways(sp, ordered, general)
            all_stored(sp, node[2], 1)

        @block.gpsimd
        def _(pool):
            def const(ins):
                ins.then_inc(s["chainp"], 1)
                const.n += 1
                pool.wait_ge(s["chainp"], const.n)
            const.n = 0
            const(nc.gpsimd.memset(prev_i[:, :], 0))
            nc.gpsimd.memset(root[:, 0:3 * TC].bitcast(I32), 0).then_inc(s["pads"], 1)
            const(nc.gpsimd.memset(ident[:, :], 0.0))
            const(nc.gpsimd.affine_select(out=ident[:, :], in_=ident[:, :], compare_op=ALU.not_equal, fill=1.0,
                                          base=0, pattern=[[-1, P]], channel_multiplier=1))
            const(nc.gpsimd.memset(ones[:, :], 1.0))
            const(nc.gpsimd.affine_select(out=tri_le[:, :], in_=ones[:, :], compare_op=ALU.is_ge, fill=0.0,
                                          base=0, pattern=[[-1, P]], channel_multiplier=1))
            const(nc.gpsimd.iota(te(edge_no), pattern=[[P * P, SL], [1, P]], base=0, channel_multiplier=P,
                                 allow_small_or_imprecise_dtypes=True))
            const(nc.gpsimd.iota(iota_row[:, :], pattern=[[1, P]], base=0, channel_multiplier=0,
                                 allow_small_or_imprecise_dtypes=True))
            nc.gpsimd.iota(iota_col[:, :], pattern=[[0, 1]], base=0, channel_multiplier=1,
                           allow_small_or_imprecise_dtypes=True).then_inc(s["consts"], 1)

            def gather(table, i, u, ring_free, staged0):
                q = i * U + u
                if u % 4 == 0:
                    pool.wait_ge(s["idx_staged"], staged0 + 2 * i + u // 4 + 1)
                if later(q, U):
                    pool.wait_ge(ring_free[0], ring_free[1] + q - U + 1)
                pool.sem_inc(s["quads_begun"], 1)
                for j in range(4):
                    nc.gpsimd.indirect_dma_start(
                        out=ring[:, u, j, :], out_offset=None, in_=table[:, :],
                        in_offset=bass.IndirectOffsetOnAxis(ap=idx_stage[:, u // 4, 4 * (u % 4) + j:4 * (u % 4) + j + 1], axis=0),
                    ).then_inc(arrived[u], 16)

            def add(l, k, v, q, base):
                pool.wait_ge(s["add_idx_ready"], base + q + 1)
                pool.wait_ge(s["sums_sb"], base + q + 1)
                for j in range(C):
                    wait_added(pool, k, v, q, base, 0, [j])
                    pool.sem_inc(s["adds_begun"], 1)
                    nc.gpsimd.indirect_dma_start(
                        out=acc_dram[l][C * (v % 2) + j][:, :],
                        out_offset=bass.IndirectOffsetOnAxis(ap=add_idx[:, v % 4, j:j + 1], axis=0),
                        in_=sums[:, v % 4, j, :], in_offset=None, compute_op=ALU.add,
                    ).then_inc(added[v % 2][j], 16)

            def sum_pairs(l):
                n, places = node[l], copies(l)
                for t in range(2 * NG):
                    c = places[t % len(places)]
                    pool.wait_ge(n[f"copies_loaded{t % len(places)}"], 16 * C * (t // len(places) + 1))
                    nc.gpsimd.tensor_tensor(c[:, 0:2], c[:, 0:2], c[:, 2:4], ALU.add).then_inc(n["pairs_summed"], 1)

            def normalise_odd_groups():
                n = node[2]
                pool.wait_ge(n["scale_done"], 1)
                for h in range(1, NG, 2):
                    normalise(nc.gpsimd, h).then_inc(n["out_done1"], 1)

            def ordered():
                pool.wait_ge(s["zero_stored"], 16 * (2 * C + 1))
                edge_steps(pool, 0, lambda i, u: add(0, i, u, i * U + u, 0))
                sum_pairs(0)
                for l, table in ((1, x1_dram), (2, h1_dram)):
                    all_stored(pool, node[l - 1])
                    edge_steps(pool, 0, lambda i, u: gather(table, i, u, (s[f"agg_ready{l}"], 0), STAGED * (l - 1)))
                normalise_odd_groups()

            def general():
                pool.wait_ge(s["zero_stored"], 16 * (6 * C + 1))
                pool.wait_ge(s["h_stored"], 16 * NG)
                for l, table in enumerate((h_dram, x1_dram, h1_dram)):
                    if l:
                        all_stored(pool, node[l - 1])

                    def step(i, u):
                        if back(i, u, 0):
                            gather(table, i, u, (s["sums_ready"], l * Q), STAGED * l)
                        c = back(i, u, 3)
                        if c:
                            add(l, *c, l * Q)
                    edge_steps(pool, 3, step)
                    sum_pairs(l)
                normalise_odd_groups()

            two_ways(pool, ordered, general)

        @block.scalar
        def _(act):
            chain = [0]

            def link(ins):
                chain[0] += 1
                ins.then_inc(s["chaina"], 1)
                act.wait_ge(s["chaina"], chain[0])

            for g in range(NG + 1):
                if g < NG:
                    act.wait_ge(s["xt_psum"], g + 1)
                    if g >= 1:
                        act.wait_ge(s["h_psum"], g)
                    nc.scalar.copy(xT, wide(g % 2)[:, 0:GW * P]).then_inc(s["xt_sb"], 1)
                if g >= 1:
                    act.wait_ge(s["h_psum"], g)
                    nc.scalar.copy(h_places[g - 1], wide(2 + (g - 1) % 2)[:, 0:GW * F]).then_inc(s["h_sb"], 1)
            for n, t in enumerate((src_idx, dst_idx, weight, slot)):
                act.wait_ge(s["te_psum"], n + 1)
                nc.scalar.copy(t[:, :], wide(n % 2)[:, 0:TC]).then_inc(s["te_sb"], 1)
            act.wait_ge(s["first_psum"], 1)
            nc.scalar.copy(first_row[:, :], wide(2)[0:1, 0:TC]).then_inc(s["first_ready"], 1)

            def stage(table, i, half, round0, seen0):
                if seen0 or later(i, 1):
                    for u in range(4 * half, 4 * half + 4):
                        act.wait_ge(arrived[u], 64 * (round0 + i))
                nc.scalar.copy(idx_stage[:, half, :], table[:, bass.ds(i * 32 + 16 * half, 16)]).then_inc(s["idx_staged"], 1)

            def stage_steps(table, round0, seen0):
                def step(i, u):
                    if u == 4:
                        stage(table, i + 1, 0, round0, seen0)
                    if u == 0 and later(i, 1):
                        stage(table, i, 1, round0, seen0)
                return step

            def radial(i, u):
                c = back(i, u, 0)
                if c:
                    _, _, q = c
                    act.wait_ge(s["ft_ready"], q + 1)
                    if later(q, 2):
                        act.wait_ge(s["z1_ready"], q - 1)
                    nc.scalar.copy(fT[0:K, u % 2, :].rearrange("k (p a) -> k a p", a=4),
                                   ps[0:K, 0, :].rearrange("k (a p) -> k a p", a=4)).then_inc(s["ft_copied"], 1)
                c = back(i, u, 1)
                if c:
                    _, v, q = c
                    z, t = ps[:, 1 + v % 2, :], soft[:, v % 2, :]
                    act.wait_ge(s["z1_ready"], q + 1)
                    if later(q, 2):
                        act.wait_ge(s["ssp_done"], q - 1)
                    nc.scalar.activation(t, z, ACT.Relu, bias=cap_col[:, :], scale=-1.0).then_inc(s["soft_done"], 1)
                    act.wait_ge(s["soft_done"], 3 * q + 1)
                    nc.scalar.activation(t, t, ACT.Exp, bias=cap_col[:, :], scale=-1.0).then_inc(s["soft_done"], 1)
                    act.wait_ge(s["soft_done"], 3 * q + 2)
                    nc.scalar.activation(t, t, ACT.Ln, bias=half_col[:, :], scale=0.5).then_inc(s["soft_done"], 1)

            def keep_sums(k, v, q, base):
                act.wait_ge(s["sums_ready"], base + q + 1)
                wait_added(act, k, v, q, base, 1)
                nc.scalar.copy(sums[:, v % 4], ps[:, 5 + v % 2, :].rearrange("p (j f) -> p j f", f=F)).then_inc(s["sums_sb"], 1)

            def ordered0(i, u):
                c = back(i, u, 5)
                if c:
                    keep_sums(*c, 0)
                radial(i, u)
                c = back(i, u, 2)
                if c:
                    _, v, q = c
                    act.wait_ge(s["rows_psum"], q + 1)
                    if later(q, 4):
                        act.wait_ge(s["sums_ready"], q - 3)
                    nc.scalar.copy(rows[:, v % 4], ps[:, 7, :].rearrange("p (j f) -> p j f", f=F)).then_inc(s["rows_sb"], 1)

            def general_step(l):
                stages = stage_steps(src_idx if l else dst_idx, NI * l, l > 0)

                def step(i, u):
                    c = back(i, u, 4)
                    if c:
                        keep_sums(*c, l * Q)
                    if l == 0:
                        radial(i, u)
                    if back(i, u, 0):
                        stages(i, u)
                return step

            def node_phase(l, summed):
                n = node[l]
                for g in range(NG + 1):
                    if summed and g < NG:
                        act.wait_ge(n["copies_summed"], 2 * (g + 1))
                        if g >= 1:
                            act.wait_ge(n["nt_psum" if l == 0 else "rows_psum"], g)
                        nc.scalar.copy(gT, wide(1)[:, 0:GW * F]).then_inc(n["agg_sb"], 1)
                    if l == 0 and g < NG:
                        act.wait_ge(n["nt_psum"], g + 1)
                        if g >= 1:
                            act.wait_ge(n["ssp"], g)
                        v = wide(2)[:, 0:GW * F]
                        link(nc.scalar.activation(nT, v, ACT.Relu, bias=cap_bo1[:, :], scale=-1.0))
                        link(nc.scalar.activation(nT, nT, ACT.Exp, bias=cap_col[:, :], scale=-1.0))
                        nc.scalar.activation(nT, nT, ACT.Ln, bias=half_col[:, :], scale=0.5).then_inc(n["nt_soft"], 1)
                    h = g - 1
                    if l == 0 and h >= 0:
                        inverse_deviation(n, h, GW)
                if l == 2:
                    inverse_deviation(n, NG - 1, NW)

            def inverse_deviation(n, h, c):
                act.wait_ge(n["var_done"], h + 1)
                link(nc.scalar.activation(rs[:, 0, 0:c], mv[:, 0:c, 1], ACT.Ln, bias=eps_col[:, :]))
                nc.scalar.activation(rs[:, 1, 0:c], rs[:, 0, 0:c], ACT.Exp, scale=-0.5).then_inc(n["rstd"], 1)

            def roots(l):
                n = node[l]
                for h in range(NG):
                    act.wait_ge(n["yt_psum"], h + 1)
                    if h >= 1:
                        act.wait_ge(n["root_psum"], h)
                    nc.scalar.copy(yT.rearrange("p w f -> p (w f)"), wide(1)[:, 0:GW * F]).then_inc(n["yt_sb"], 1)
                    act.wait_ge(n["root_psum"], h + 1)
                    if l == 1 and h == 0:
                        all_stored(act, n)
                    nc.scalar.copy(root[:, h * GW * F:(h + 1) * GW * F], wide(3)[:, 0:GW * F]).then_inc(n["root_done"], 1)

            def ordered():
                act.wait_ge(s["te_sb"], 4)
                edge_steps(act, 5, ordered0)
                stage(src_idx, 0, 0, 0, False)
                stage(src_idx, 0, 1, 0, False)
                node_phase(0, True)
                roots(0)
                edge_steps(act, 0, stage_steps(src_idx, 0, False))
                next_first(1)
                node_phase(1, False)
                roots(1)
                edge_steps(act, 0, stage_steps(src_idx, NI, True))
                node_phase(2, False)

            def next_first(rounds):
                for half in range(2):
                    for u in range(4 * half, 4 * half + 4):
                        act.wait_ge(arrived[u], 64 * NI * rounds)
                    act.wait_ge(s["idx_staged"], STAGED * rounds + half)
                    nc.scalar.copy(idx_stage[:, half, :], src_idx[:, 16 * half:16 * half + 16]).then_inc(s["idx_staged"], 1)

            def general():
                act.wait_ge(s["te_sb"], 4)
                stage(dst_idx, 0, 0, 0, False)
                stage(dst_idx, 0, 1, 0, False)
                edge_steps(act, 4, general_step(0))
                next_first(1)
                node_phase(0, True)
                roots(0)
                edge_steps(act, 4, general_step(1))
                next_first(2)
                node_phase(1, True)
                roots(1)
                edge_steps(act, 4, general_step(2))
                node_phase(2, True)

            two_ways(act, ordered, general, chain)

        @block.vector
        def _(dve):
            chain = [0]

            def then_chain(ins):
                chain[0] += 1
                ins.then_inc(s["chainv"], 1)

            def link(ins):
                then_chain(ins)
                dve.wait_ge(s["chainv"], chain[0])

            nc.vector.memset(x_sb[:, NW - 1, :], 0.0).then_inc(s["x_pad"], 1)
            nc.vector.memset(aggT[:, :], 0.0).then_inc(s["zeroed"], 1)
            for t, value in ((cap_col[:, :], CAP), (half_col[:, :], 0.5), (eps_col[:, :], EPS), (ones3[:, :], 1.0), (fT[:, :, :], 1.0)):
                then_chain(nc.vector.memset(t, value))
            dve.wait_ge(s["consts"], 1)
            dve.wait_ge(s["w_loads"], 16 * 16)
            link(nc.vector.tensor_copy(bpart[0], bias3))
            link(nc.vector.tensor_tensor(bres[0], bias3, bpart[0], ALU.subtract))
            link(nc.vector.tensor_copy(bpart[1], bres[0]))
            link(nc.vector.tensor_tensor(bres[1], bres[0], bpart[1], ALU.subtract))
            link(nc.vector.tensor_copy(bpart[2], bres[1]))
            for r in range(3):
                link(nc.vector.tensor_scalar(pick[:, r:r + 1], iota_col[0:3, :], float(r), None, ALU.is_equal))
            link(nc.vector.tensor_scalar(bpart[0], bpart[0], pick[:, 0:1], None, ALU.mult))
            link(nc.vector.scalar_tensor_tensor(bpart[0], bpart[1], pick[:, 1:2], bpart[0], ALU.mult, ALU.add))
            link(nc.vector.scalar_tensor_tensor(bpart[0], bpart[2], pick[:, 2:3], bpart[0], ALU.mult, ALU.add))
            for r in range(4):
                then_chain(nc.vector.tensor_copy(brow[:, :, r, :], bpart[0]))
            then_chain(nc.vector.tensor_scalar(cap_bo1[:, :], bo1c[:, :], -1.0, CAP, ALU.mult, ALU.add))
            nc.vector.tensor_scalar(bo1_log2[:, :], bo1c[:, :], -LOG2, None, ALU.add).then_inc(s["bias_ready"], 1)
            dve.wait_ge(s["te_loads"], 16 * (9 + SL))
            then_chain(nc.vector.tensor_scalar(valid, edge_no, float(E), None, ALU.is_lt))
            then_chain(nc.vector.tensor_copy(prev_f[:, :], prev_i[:, :]))
            then_chain(nc.vector.tensor_copy(src_te, src_i))
            link(nc.vector.tensor_copy(dst_te, dst_i))
            link(nc.vector.memset(prev_f[0:1, 0:1], -1.0))
            d3 = te(dst_te)
            link(nc.vector.tensor_tensor(te(rel_te), d3, d3[:, :, 0:1].broadcast_to([P, SL, P]), ALU.subtract))
            nc.vector.tensor_copy(rel_bf, rel_te).then_inc(s["rel_sb"], 1)
            then_chain(nc.vector.tensor_tensor(te(diff)[:, :, 1:P], d3[:, :, 1:P], d3[:, :, 0:P - 1], ALU.subtract))
            link(nc.vector.tensor_tensor(te(diff)[:, :, 0], d3[:, :, 0], prev_f[:, :], ALU.subtract))
            link(nc.vector.tensor_tensor(diff, diff, valid, ALU.mult))
            link(nc.vector.scalar_tensor_tensor(viol, diff, -1.0, diff, ALU.add, ALU.mult))
            link(nc.vector.tensor_reduce(flag_f[:, 0:1], diff, AX.X, ALU.add))
            nc.vector.tensor_reduce(flag_f[:, 1:2], viol, AX.X, ALU.add).then_inc(s["te_ready"], 1)
            dve.wait_ge(s["te_ready"], 1)
            dve.wait_ge(s["flag_psum"], 1)
            link(nc.vector.tensor_scalar(flag_f[:, 2:3], ps[:, 6, 0:1], float(N), None, ALU.is_equal))
            link(nc.vector.tensor_scalar(flag_f[:, 3:4], ps[:, 6, 1:2], 0.0, None, ALU.is_equal))
            nc.vector.tensor_tensor(flag[0:1, 0:1], flag_f[0:1, 2:3], flag_f[0:1, 3:4], ALU.mult).then_inc(s["flag_ready"], 1)
            link(nc.vector.tensor_scalar(tail_col[:, 0:1], iota_col[:, :], float(REST), None, ALU.is_lt))
            link(nc.vector.tensor_scalar(tail_col[:, 1:2], tail_col[:, 0:1], -1.0, None, ALU.add))
            link(nc.vector.tensor_scalar(tail_col[:, 2:3], iota_col[:, :], float(N), None, ALU.add))

            def end_with_minus_one(t):
                link(nc.vector.tensor_scalar(t[:, FULLT:FULLT + 1], t[:, FULLT:FULLT + 1], tail_col[:, 0:1], tail_col[:, 1:2], ALU.mult, ALU.add))
                link(nc.vector.memset(t[:, FULLT + 1:TC], -1.0))

            def make_spare(col):
                link(nc.vector.tensor_scalar(spare[:, :], col[:, :], -1.0, tail_col[:, 2:3], ALU.mult, ALU.add))

            dve.wait_ge(s["te_sb"], 1)
            link(nc.vector.tensor_copy(src_col[:, :], src_idx[:, :]))
            end_with_minus_one(src_col)
            make_spare(src_col)
            dve.wait_ge(s["wt_psum"], 1)
            nc.vector.tensor_copy(wT[:, :, :].rearrange("p a f -> p (a f)"), ps[:, 6, :]).then_inc(s["wt_sb"], 1)

            def late_tables():
                dve.wait_ge(s["te_sb"], 4)
                hi = dst_hi[:, :].bitcast(I32)
                lo = dst_lo[:, :].bitcast(I32)
                link(nc.vector.tensor_copy(dst_col[:, :], dst_idx[:, :]))
                link(nc.vector.tensor_scalar(hi, dst_idx[:, :], 7, None, ALU.arith_shift_right))
                link(nc.vector.tensor_scalar(lo, dst_idx[:, :], P - 1, None, ALU.bitwise_and))
                link(nc.vector.tensor_copy(dst_hi[:, :], hi))
                link(nc.vector.tensor_copy(dst_lo[:, :], lo))
                end_with_minus_one(dst_lo)
                end_with_minus_one(dst_col)
                end_with_minus_one(slot)

            def equal_keys(k, v, q, col, base):
                dve.wait_ge(s[f"key_loaded{v // 2 % 2}"], 16 * (base // 4 + 2 * k + v // 4 + 1))
                if base or later(q, 4):
                    dve.wait_ge(s["sums_ready"], base + q - 3)
                for j in range(4):
                    ins = nc.vector.scalar_tensor_tensor(
                        hot[:, v % 4, j, :], key_row[:, v % 4, j * P:(j + 1) * P], col[:, bass.ds(4 * q + j, 1)],
                        tri_le[:, :], ALU.is_equal, ALU.mult, accum_out=rank[:, v % 2, j:j + 1])
                ins.then_inc(s["same_ready"], 1)
                dve.wait_ge(s["same_ready"], base + q + 1)
                nc.vector.scalar_tensor_tensor(other[:, v % 2, :], rank[:, v % 2, :], 1.0, spare[:, bass.ds(4 * q, 4)],
                                               ALU.not_equal, ALU.mult).then_inc(s["other_ready"], 1)
                dve.wait_ge(s["other_ready"], base + q + 1)
                wait_added(dve, k, v, q, base, 1)
                nc.vector.tensor_tensor(add_idx[:, v % 4, :], other[:, v % 2, :], col[:, bass.ds(4 * q, 4)],
                                        ALU.add).then_inc(s["add_idx_ready"], 1)

            def ssp(i, u):
                c = back(i, u, 1)
                if c:
                    _, v, q = c
                    dve.wait_ge(s["soft_done"], 3 * q + 3)
                    if later(q, 2):
                        dve.wait_ge(s["z2_ready"], q - 1)
                    nc.vector.scalar_tensor_tensor(act_s[:, v % 2, :], ps[:, 1 + v % 2, :], -LOG2, soft[:, v % 2, :],
                                                   ALU.add, ALU.max).then_inc(s["ssp_done"], 1)

            def messages(v, q, rows_at):
                dve.wait_ge(s["z2_ready"], q + 1)
                for j in range(4):
                    xj = rows_at[:, j, :]
                    ins = nc.vector.scalar_tensor_tensor(xj, ps[:, 3 + v % 2, j * P:(j + 1) * P],
                                                         weight[:, bass.ds(4 * q + j, 1)], xj, ALU.mult, ALU.mult)
                ins.then_inc(s["x_ready"], 1)

            def ordered0(i, u):
                c = back(i, u, 3)
                if c:
                    _, v, q = c
                    dve.wait_ge(s["rows_sb"], q + 1)
                    messages(v, q, rows[:, v % 4])
                c = back(i, u, 1)
                if c:
                    k, v, q = c
                    dve.wait_ge(s[f"rel_loaded{v // 2 % 2}"], 16 * (2 * k + v // 4 + 1))
                    if later(q, 2):
                        dve.wait_ge(s["rows_psum"], q - 1)
                    nc.vector.tensor_scalar(spread[:, v % 2, :], rel_row[:, v % 4, :], iota_col[:, :], None,
                                            ALU.is_equal).then_inc(s["spread_ready"], 1)
                ssp(i, u)
                c = back(i, u, 2)
                if c:
                    equal_keys(*c, src_col, 0)

            def histogram(v, q, table_lo, table_hi):
                if later(q, 2):
                    dve.wait_ge(s["hist_used"], q - 1)
                for j in range(4):
                    nc.vector.tensor_scalar(lo_hot[:, v % 2, j, :], iota_row[:, :], table_lo[:, bass.ds(4 * q + j, 1)], None, ALU.is_equal)
                    ins = nc.vector.tensor_scalar(hi_hot[:, v % 2, j, :], iota_row[:, 0:NW], table_hi[:, bass.ds(4 * q + j, 1)], None, ALU.is_equal)
                ins.then_inc(s["hist_ready"], 1)

            def counts():
                dve.wait_ge(s["hist_used"], Q)
                link(nc.vector.tensor_scalar(rcnt[:, 0, :], ps[:, 7, 0:NW], 1.0, None, ALU.max))
                nc.vector.reciprocal(rcnt[:, 1, :], rcnt[:, 0, :]).then_inc(s["cnt_ready"], 1)
                dve.wait_ge(s["cnt_ready"], 1)

            dve_regs = [dve.alloc_register(f"dve_first{j}") for j in range(4)]

            def ordered12(l):
                hot_ready, agg_ready, acc_done = s[f"hot_ready{l}"], s[f"agg_ready{l}"], s[f"acc_done{l}"]

                def step(i, u):
                    c = back(i, u, 0)
                    if c:
                        _, v, q = c
                        if later(q, 2):
                            dve.wait_ge(agg_ready, q - 1)
                        for j in range(4):
                            ins = nc.vector.tensor_scalar(hot[:, v % 2, j, :], iota_row[:, :], slot[:, bass.ds(4 * q + j, 1)],
                                                          None, ALU.is_equal)
                        ins.then_inc(hot_ready, 1)
                        if l == 1:
                            histogram(v, q, dst_lo, dst_hi)
                    c = back(i, u, 1)
                    if c:
                        _, v, q = c
                        firsts = load_firsts(dve, dve_regs, q)
                        dve.wait_ge(agg_ready, q + 1)
                        for j in range(4):
                            if j or later(q, 1):
                                dve.wait_ge(acc_done, 4 * q + j)
                            a = aggT[:, bass.ds(firsts[j], P)]
                            nc.vector.tensor_tensor(a, ps[:, 5 + v % 2, j * P:(j + 1) * P], a, ALU.add).then_inc(acc_done, 1)
                edge_steps(dve, 1, step)

            def moments(yw, w0):
                for j in range(GW):
                    ins = nc.vector.bn_stats(stats[:, w0 + j, :], yw[:, j, :])
                link(ins)
                for j in range(GW):
                    ins = nc.vector.bn_aggr(mv[:, w0 + j, :], stats[:, w0 + j, :])
                return ins

            def newton(c):
                r = rs[:, 1, 0:c]
                link(nc.vector.tensor_tensor(rs[:, 2, 0:c], r, r, ALU.mult))
                link(nc.vector.scalar_tensor_tensor(rs[:, 3, 0:c], mv[:, 0:c, 1], EPS, rs[:, 2, 0:c], ALU.add, ALU.mult))
                link(nc.vector.tensor_scalar(rs[:, 3, 0:c], rs[:, 3, 0:c], -0.5, 1.5, ALU.mult, ALU.add))
                return nc.vector.tensor_tensor(rs[:, 2, 0:c], r, rs[:, 3, 0:c], ALU.mult)

            def node_phase0():
                n = node[0]
                for g in range(NG + 1):
                    if g < NG:
                        dve.wait_ge(n["nt_soft"], g + 1)
                        if g >= 2:
                            dve.wait_ge(n["out_psum"], g - 1)
                        nc.vector.scalar_tensor_tensor(nS[:, g % 2, :], wide(2)[:, 0:GW * F], bo1_log2[:, :], nT,
                                                       ALU.add, ALU.max).then_inc(n["ssp"], 1)
                    h = g - 1
                    if h >= 0:
                        xw, yw = x_sb[:, h * GW:(h + 1) * GW, :], yv[:, h % 2]
                        dve.wait_ge(n["out_psum"], h + 1)
                        nc.vector.tensor_tensor(yw, windows(wide(0)[:, 0:GW * F]), xw, ALU.add).then_inc(n["sum_done"], 1)
                        dve.wait_ge(n["sum_done"], h + 1)
                        moments(yw, 0).then_inc(n["var_done"], 1)
                        dve.wait_ge(n["rstd"], h + 1)
                        link(newton(GW))
                        for j in range(GW):
                            ins = nc.vector.tensor_scalar(xw[:, j, :], yw[:, j, :], mv[:, j, 0:1], rs[:, 2, j:j + 1],
                                                          ALU.subtract, ALU.mult)
                        ins.then_inc(n["y_done"], 1)
                        dve.wait_ge(n["y_done"], h + 1)

            def node_phase(l):
                n = node[l]
                for h in range(NG):
                    yw = windows(root[:, h * GW * F:(h + 1) * GW * F])
                    dve.wait_ge(n["rows_psum"], h + 1)
                    for j in range(GW):
                        w = h * GW + j
                        ins = nc.vector.scalar_tensor_tensor(yw[:, j, :], wide(2 * (h % 2))[:, j * F:(j + 1) * F], rcnt[:, 1, w:w + 1],
                                                             yw[:, j, :], ALU.mult, ALU.add)
                    ins.then_inc(n["row_done"], 1)
                    dve.wait_ge(n["row_done"], h + 1)
                    if l == 1:
                        nc.vector.tensor_scalar(yw, yw, 0.0, None, ALU.max).then_inc(n["y_done"], 1)
                    else:
                        link(nc.vector.scalar_tensor_tensor(yw, yw, 0.0, x_sb[:, h * GW:(h + 1) * GW, :], ALU.max, ALU.add))
                        moments(yw, h * GW).then_inc(n["var_done"], 1)
                if l == 2:
                    dve.wait_ge(n["rstd"], 1)
                    newton(NW).then_inc(n["scale_done"], 1)
                    dve.wait_ge(n["scale_done"], 1)
                    for h in range(0, NG, 2):
                        normalise(nc.vector, h).then_inc(n["out_done0"], 1)

            def clear_agg(l):
                dve.wait_ge(node[l]["rows_psum" if l else "copies_summed"], NG if l else 2 * NG)
                if l == 0:
                    dve.wait_ge(node[0]["ssp"], NG)
                nc.vector.memset(aggT[:, :], 0.0).then_inc(s[f"agg_clear{l + 1}"], 1)
                dve.wait_ge(s[f"agg_clear{l + 1}"], 1)

            def ordered():
                late_tables()
                edge_steps(dve, 3, ordered0)
                node_phase0()
                clear_agg(0)
                ordered12(1)
                counts()
                node_phase(1)
                clear_agg(1)
                ordered12(2)
                node_phase(2)

            def general():
                late_tables()
                general_edges(0)
                node_phase0()
                make_spare(dst_col)
                general_edges(1)
                counts()
                node_phase(1)
                general_edges(2)
                node_phase(2)

            def general_edges(l):
                def step(i, u):
                    if l == 0:
                        ssp(i, u)
                    c = back(i, u, 2)
                    if c:
                        k, v, q = c
                        equal_keys(k, v, q, dst_col if l else src_col, l * Q)
                        if l == 1:
                            histogram(v, q, dst_lo, dst_hi)
                        if l == 0:
                            dve.wait_ge(arrived[v], 64 * (k + 1))
                            messages(v, q, ring[:, v])
                edge_steps(dve, 2, step)

            two_ways(dve, ordered, general, chain)

        @block.tensor
        def _(pe):
            def bias(out_ap, n):
                c = out_ap.shape[-1]
                for b in range(0, c, 512):
                    w = min(512, c - b)
                    nc.tensor.matmul(out_ap[:, b:b + w], ones3[:, :],
                                     brow[:, n, :, :].rearrange("r a f -> r (a f)")[:, 0:w],
                                     start=True, stop=False, skip_group_check=True)

            pe.wait_ge(s["consts"], 1)
            pe.wait_ge(s["w_loads"], 16 * 16)
            for g in range(NG):
                pe.wait_ge(x_loaded[g], 16 if g < NG - 1 else 32)
                if g >= 2:
                    pe.wait_ge(s["xt_sb"], g - 1)
                for j in range(GW):
                    ins = nc.tensor.transpose(wide(g % 2)[:, j * P:(j + 1) * P], x_sb[:, g * GW + j, :], ident[:, :])
                ins.then_inc(s["xt_psum"], 1)
                if g == 0:
                    pe.wait_ge(s["bias_ready"], 1)
                pe.wait_ge(s["xt_sb"], g + 1)
                if g >= 2:
                    pe.wait_ge(s["h_sb"], g - 1)
                hp = wide(2 + g % 2)
                bias(hp[:, 0:GW * F], 0)
                for j in range(GW):
                    ins = nc.tensor.matmul(hp[:, j * F:(j + 1) * F], xT[:, j * P:(j + 1) * P], w_in[:, :],
                                           start=False, stop=True, skip_group_check=True)
                ins.then_inc(s["h_psum"], 1)
            pe.wait_ge(s["h_sb"], NG)
            pe.wait_ge(s["te_ready"], 1)
            nc.tensor.matmul(ps[:, 6, 0:2], ones[:, :], flag_f[:, 0:2], start=True, stop=True).then_inc(s["flag_psum"], 1)
            for n, v in enumerate((src_te, dst_te, ew_te, rel_te)):
                if n >= 2:
                    pe.wait_ge(s["te_sb"], n - 1)
                for k in range(SL):
                    ins = nc.tensor.transpose(wide(n % 2)[:, k * P:(k + 1) * P], v[:, k * P:(k + 1) * P], ident[:, :])
                ins.then_inc(s["te_psum"], 1)
            for k in range(SL):
                ins = nc.tensor.transpose(wide(2)[0:1, k * P:(k + 1) * P], dst_te[:, k * P:k * P + 1], ident[:, :])
            ins.then_inc(s["first_psum"], 1)
            pe.wait_ge(s["flag_ready"], 1)
            for k in range(4):
                ins = nc.tensor.transpose(ps[:, 6, k * P:(k + 1) * P], wraw[:, k, :], ident[:, :])
            ins.then_inc(s["wt_psum"], 1)
            pe.wait_ge(s["te_sb"], 4)
            pe.wait_ge(s["first_ready"], 1)
            pe.wait_ge(s["wt_sb"], 1)

            def radial(i, u):
                c = back(i, u, 0)
                if c:
                    k, v, q = c
                    pe.wait_ge(f_loaded[v - v % 2], 16 * (k + 1))
                    if later(q, 1):
                        pe.wait_ge(s["ft_copied"], q)
                    for j in range(4):
                        ins = nc.tensor.transpose(ps[0:K, 0, j * P:(j + 1) * P], f_sb[:, v, j * K:(j + 1) * K], ident[:, :])
                    ins.then_inc(s["ft_ready"], 1)
                c = back(i, u, 1)
                if c:
                    _, v, q = c
                    pe.wait_ge(s["ft_copied"], q + 1)
                    if later(q, 2):
                        pe.wait_ge(s["ssp_done"], q - 1)
                    nc.tensor.matmul(ps[:, 1 + v % 2, :], wf1[:, :], fT[:, v % 2, :], start=True, stop=True).then_inc(s["z1_ready"], 1)
                c = back(i, u, 2)
                if c:
                    _, v, q = c
                    pe.wait_ge(s["ssp_done"], q + 1)
                    if later(q, 2):
                        pe.wait_ge(s["x_ready"], q - 1)
                    z = ps[:, 3 + v % 2, :]
                    bias(z, 1)
                    for j in range(4):
                        ins = nc.tensor.matmul(z[:, j * F:(j + 1) * F], act_s[:, v % 2, j * P:(j + 1) * P], wf2[:, :],
                                               start=False, stop=True, skip_group_check=True)
                    ins.then_inc(s["z2_ready"], 1)

            def sum_keys(v, q, base, rows_at):
                pe.wait_ge(s["same_ready"], base + q + 1)
                if base or later(q, 2):
                    pe.wait_ge(s["sums_sb"], base + q - 1)
                for j in range(4):
                    ins = nc.tensor.matmul(ps[:, 5 + v % 2, j * P:(j + 1) * P], hot[:, v % 4, j, :], rows_at[:, j, :],
                                           start=True, stop=True)
                ins.then_inc(s["sums_ready"], 1)

            def ordered0(i, u):
                radial(i, u)
                c = back(i, u, 2)
                if c:
                    k, v, q = c
                    pe.wait_ge(s["spread_ready"], q + 1)
                    pe.wait_ge(windows_loaded[v], 64 * (k + 1))
                    if later(q, 1):
                        pe.wait_ge(s["rows_sb"], q)
                    for j in range(4):
                        ins = nc.tensor.matmul(ps[:, 7, j * F:(j + 1) * F], spread[:, v % 2, j * P:(j + 1) * P], ring[:, v, j, :],
                                               start=True, stop=True)
                    ins.then_inc(s["rows_psum"], 1)
                c = back(i, u, 4)
                if c:
                    _, v, q = c
                    pe.wait_ge(s["x_ready"], q + 1)
                    sum_keys(v, q, 0, rows[:, v % 4])

            def count(v, q):
                pe.wait_ge(s["hist_ready"], q + 1)
                for j in range(4):
                    ins = nc.tensor.matmul(ps[:, 7, 0:NW], lo_hot[:, v % 2, j, :], hi_hot[:, v % 2, j, :],
                                           start=not later(q, 1) and j == 0, stop=False, skip_group_check=True)
                ins.then_inc(s["hist_used"], 1)

            def ordered12(l):
                hot_ready, agg_ready, acc_done = s[f"hot_ready{l}"], s[f"agg_ready{l}"], s[f"acc_done{l}"]

                def step(i, u):
                    q = i * U + u
                    pe.wait_ge(hot_ready, q + 1)
                    if later(q, 2):
                        pe.wait_ge(acc_done, 4 * (q - 1))
                    pe.wait_ge(arrived[u], 64 * (NI * (l - 1) + i + 1))
                    for j in range(4):
                        ins = nc.tensor.matmul(ps[:, 5 + u % 2, j * P:(j + 1) * P], ring[:, u, j, :], hot[:, u % 2, j, :],
                                               start=True, stop=True)
                    ins.then_inc(agg_ready, 1)
                    if l == 1:
                        count(u, q)
                edge_steps(pe, 0, step)
                pe.wait_ge(acc_done, TP)

            def general_edges(l):
                def step(i, u):
                    if l == 0:
                        radial(i, u)
                    c = back(i, u, 3)
                    if c:
                        k, v, q = c
                        if l == 0:
                            pe.wait_ge(s["x_ready"], q + 1)
                        else:
                            pe.wait_ge(arrived[v], 64 * (NI * l + k + 1))
                        if l == 1:
                            count(v, q)
                        sum_keys(v, q, l * Q, ring[:, v])
                edge_steps(pe, 3, step)

            def node_phase(l, summed):
                n = node[l]
                for g in range(NG + 1):
                    if summed and g < NG:
                        if g >= 1:
                            pe.wait_ge(n["agg_sb"], g)
                        for b in range(2):
                            t, places = 2 * g + b, copies(l)
                            pe.wait_ge(n["pairs_summed"], t + 1)
                            for j in range(GW):
                                for k in range(2):
                                    ins = nc.tensor.matmul(wide(1)[:, j * P:(j + 1) * P], places[t % len(places)][:, k, j, :], ident[:, :],
                                                           start=b == 0 and k == 0 and j % 4 == 0, stop=b == 1 and k == 1,
                                                           skip_group_check=True)
                            ins.then_inc(n["copies_summed"], 1)
                        pe.wait_ge(n["agg_sb"], g + 1)
                    if l == 0 and g < NG:
                        if g >= 1:
                            pe.wait_ge(n["ssp"], g)
                        nc.tensor.matmul(wide(2)[:, 0:512], wo1[:, :], gT[:, 0:512], start=True, stop=True)
                        nc.tensor.matmul(wide(2)[:, 512:GW * F], wo1[:, :], gT[:, 512:GW * F], start=True, stop=True).then_inc(n["nt_psum"], 1)
                    if l and g < NG:
                        if g >= 2:
                            pe.wait_ge(n["row_done"], g - 1)
                        for j in range(GW):
                            w = g * GW + j
                            lhsT = gT[:, j * P:(j + 1) * P] if summed else aggT[:, w * P:(w + 1) * P]
                            ins = nc.tensor.matmul(wide(2 * (g % 2))[:, j * F:(j + 1) * F], lhsT, wT[:, 2 * l - 2, :],
                                                   start=True, stop=True)
                        ins.then_inc(n["rows_psum"], 1)
                    h = g - 1
                    if l == 0 and 0 <= h < NG:
                        pe.wait_ge(n["ssp"], h + 1)
                        if h >= 1:
                            pe.wait_ge(n["sum_done"], h)
                        bias(wide(0)[:, 0:GW * F], 2)
                        for j in range(GW):
                            ins = nc.tensor.matmul(wide(0)[:, j * F:(j + 1) * F], nS[:, h % 2, j * P:(j + 1) * P], wo2[:, :],
                                                   start=False, stop=True, skip_group_check=True)
                        ins.then_inc(n["out_psum"], 1)

            def roots(l, summed):
                n = node[l]
                if summed:
                    pe.wait_ge(n["agg_sb"], NG)
                for h in range(NG):
                    pe.wait_ge(n["y_done"], h + 1)
                    if h >= 1:
                        pe.wait_ge(n["yt_sb"], h)
                    for j in range(GW):
                        w = h * GW + j
                        y = x_sb[:, w, :] if l == 0 else root[:, w * F:(w + 1) * F]
                        ins = nc.tensor.transpose(wide(1)[:, j * P:(j + 1) * P], y, ident[:, :])
                    ins.then_inc(n["yt_psum"], 1)
                    pe.wait_ge(n["yt_sb"], h + 1)
                    if h >= 1:
                        pe.wait_ge(n["root_done"], h)
                    if l == 1:
                        pe.wait_ge(s["cnt_ready"], 1)
                    bias(wide(3)[:, 0:GW * F], 3 + l)
                    for j in range(GW):
                        ins = nc.tensor.matmul(wide(3)[:, j * F:(j + 1) * F], yT[:, j, :], wT[:, 1 + 2 * l, :],
                                               start=False, stop=True, skip_group_check=True)
                    ins.then_inc(n["root_psum"], 1)
                pe.wait_ge(n["root_done"], NG)

            def ordered():
                edge_steps(pe, 4, ordered0)
                node_phase(0, True)
                roots(0, True)
                ordered12(1)
                node_phase(1, False)
                roots(1, False)
                ordered12(2)
                node_phase(2, False)

            def general():
                for l in range(3):
                    general_edges(l)
                    node_phase(l, True)
                    if l < 2:
                        roots(l, True)

            two_ways(pe, ordered, general)


_INS = ["x", "src", "dst", "edge_attr_20", "edge_weight"] + [f"L0_gnn_{n}" for n in (
    "W_in", "b_in", "Wf1", "bf1", "Wf2", "bf2", "Wo1", "bo1", "Wo2", "bo2")] + [
    f"L1_gnn_{n}" for n in ("Wl1", "bl1", "Wr1", "Wl2", "bl2", "Wr2")]


def kernel(**inputs):
    import concourse.bacc as bacc
    from concourse.bass_utils import run_bass_kernel_spmd

    nc = bacc.Bacc("TRN2", target_bir_lowering=False, num_devices=1)
    arrays, args = {}, []
    for name in _INS:
        a = np.ascontiguousarray(inputs[name])
        arrays[f"in_{name}"] = a
        args.append(nc.dram_tensor(f"in_{name}", a.shape, mybir.dt.from_np(a.dtype), kind="ExternalInput").ap())
    shape = inputs["x"].shape
    args.append(nc.dram_tensor("out_0", shape, F32, kind="ExternalOutput").ap())
    gnn_program(nc, *args)
    r = run_bass_kernel_spmd(nc, [arrays], core_ids=[0])
    return r.results[0]["out_0"]
```
